# Optimizing a Trainium2 kernel written in Bass

```python
import numpy as np
import jax
import jax.numpy as jnp

def _softmax(x, axis=-1):
    return jax.nn.softmax(x, axis=axis)

def _gelu(x):
    return jax.nn.gelu(x, approximate=True)

def _silu(x):
    return jax.nn.silu(x)

def _sigmoid(x):
    return jax.nn.sigmoid(x)

def _layernorm(x, axis=-1, eps=1e-05):
    m = jnp.mean(x, axis=axis, keepdims=True)
    v = jnp.var(x, axis=axis, keepdims=True)
    return (x - m) / jnp.sqrt(v + eps)

def _scatter_add(tgt, idx, src, axis=0):
    return tgt.at[idx].add(src)

def _segment_sum(src, seg, n):
    return jax.ops.segment_sum(src, seg, n)
kernel_name = 'mk_audio_tower_d1_tok_audfeat768_r4_d629cf'

def setup_inputs(seed: int=0):
    np.random.seed(seed)
    _w = jnp.asarray

    def _rec_inputs():
        import jax
        import jax.numpy as jnp
        _rk = jax.random.key(seed)
        x = -4.65018e-05 + 0.999886 * jax.random.normal(jax.random.fold_in(_rk, 1), (64, 375, 192), jnp.float32)
        return x
    x = _rec_inputs()

    def _L0_tok_setup():
        import jax, jax.numpy as jnp
        import numpy as np
        POOL_SIZE = 2
        STRIDE = 2
        CHANNELS = 192
        key = jax.random.key(seed)
        k1, = jax.random.split(key, 1)
        x = jax.random.normal(k1, (8, 2048, CHANNELS), dtype=jnp.float32)
        w = jnp.eye(CHANNELS, dtype=jnp.float32) * 2.0
        return {'x': x, 'w': w}
    _L0_tok_all = _L0_tok_setup()
    _L0_tok_in = {k: v for k, v in _L0_tok_all.items() if k in ('w',)}
    del _L0_tok_all

    def _L0_attn_setup():
        import jax, jax.numpy as jnp
        import numpy as np
        NUM_HEADS = 12
        S_BITS = 4
        ZP = 128.0

        def fq_act(t, s):
            q = jnp.clip(jnp.round(t / s) + ZP, 0.0, 255.0)
            return (q - ZP) * s

        def fq_weight(w, s):
            sc = s[:, None]
            return jnp.clip(jnp.round(w / sc), -128.0, 127.0) * sc

        def log_int_softmax(x, scale, bits=S_BITS):
            x_int = x / scale
            x_int = x_int - jnp.max(x_int, axis=-1, keepdims=True)
            n = 30.0
            x0_int = jnp.floor(-0.6931 / scale)
            x_int = jnp.maximum(x_int, n * x0_int)
            q = jnp.floor(x_int / x0_int)
            r = x_int - x0_int * q
            c0 = 0.35815147
            b_int = jnp.floor(0.96963238 / c0 / scale)
            c_int = jnp.floor(1.0 / c0 / (scale * scale))
            z = r * (r + b_int) + c_int
            exp_int = jnp.maximum(jnp.floor(z * jnp.exp2(n - q)), 0.0)
            exp_sum = jnp.sum(exp_int, axis=-1, keepdims=True)
            ratio = jnp.round(exp_sum / jnp.maximum(exp_int, 1.0))
            big = jnp.floor(jnp.log2(ratio))
            big = big + jnp.where(ratio - jnp.exp2(big) >= jnp.exp2(big - 1.0), 1.0, 0.0)
            qmax = 2.0 ** bits
            out = jnp.exp2(-jnp.clip(big, 0.0, qmax - 1.0))
            return jnp.where((big >= qmax) | (exp_int == 0.0), 0.0, out)
        key = jax.random.key(seed)
        ks = jax.random.split(key, 5)
        B, N, C = (32, 197, 192)
        x = jax.random.normal(ks[0], (B, N, C), jnp.float32)
        w_qkv = jax.random.normal(ks[1], (3 * C, C), jnp.float32) * 0.02
        b_qkv = jax.random.normal(ks[2], (3 * C,), jnp.float32) * 0.02
        w_proj = jax.random.normal(ks[3], (C, C), jnp.float32) * 0.02
        b_proj = jax.random.normal(ks[4], (C,), jnp.float32) * 0.02
        sw_qkv = jnp.max(jnp.abs(w_qkv), axis=1) / 127.0
        sw_proj = jnp.max(jnp.abs(w_proj), axis=1) / 127.0
        s_a1 = jnp.array([4.4 / 255.0], jnp.float32)
        s_attn = jnp.array([3.0 / 255.0], jnp.float32)
        s_a2 = jnp.array([1.0 / 255.0], jnp.float32)
        s_a3 = jnp.array([0.25 / 255.0], jnp.float32)
        return {'x': x, 'w_qkv': w_qkv, 'b_qkv': b_qkv, 'w_proj': w_proj, 'b_proj': b_proj, 'sw_qkv': sw_qkv, 'sw_proj': sw_proj, 's_a1': s_a1, 's_attn': s_attn, 's_a2': s_a2, 's_a3': s_a3}
    _L0_attn_all = _L0_attn_setup()
    _L0_attn_in = {k: v for k, v in _L0_attn_all.items() if k in ('w_qkv', 'b_qkv', 'w_proj', 'b_proj', 'sw_qkv', 'sw_proj', 's_a1', 's_attn', 's_a2', 's_a3')}
    del _L0_attn_all

    def _L0_ffn_setup():
        import jax, jax.numpy as jnp
        import numpy as np
        B, S, H = (2, 256, 192)
        E, K, I = (16, 4, 192)
        ALPHA, LIMIT, EPS = (1.702, 7.0, 1e-05)

        def _swiglu(h):
            x_glu, x_lin = jnp.split(h, 2, axis=-1)
            x_glu = jnp.minimum(x_glu, LIMIT)
            x_lin = jnp.clip(x_lin, -LIMIT, LIMIT)
            return x_glu * jax.nn.sigmoid(ALPHA * x_glu) * (x_lin + 1.0)
        key = jax.random.key(seed)
        ks = jax.random.split(key, 7)
        x = jax.random.normal(ks[0], (B, S, H), dtype=jnp.float32)
        scale = jnp.ones((H,), jnp.float32)
        gate_w = jax.random.normal(ks[1], (E, H), jnp.float32) * 0.02
        gate_b = jnp.zeros((E,), jnp.float32)
        w1 = jax.random.normal(ks[2], (E, H, 2 * I), jnp.float32) * 0.02
        b1 = jax.random.normal(ks[3], (E, 2 * I), jnp.float32) * 0.02
        w2 = jax.random.normal(ks[4], (E, I, H), jnp.float32) * 0.02
        b2 = jax.random.normal(ks[5], (E, H), jnp.float32) * 0.02
        return {'x': x, 'scale': scale, 'gate_w': gate_w, 'gate_b': gate_b, 'w1': w1, 'b1': b1, 'w2': w2, 'b2': b2}
    _L0_ffn_all = _L0_ffn_setup()
    _L0_ffn_in = {k: v for k, v in _L0_ffn_all.items() if k in ('scale', 'gate_w', 'gate_b', 'w1', 'b1', 'w2', 'b2')}
    del _L0_ffn_all
    return {'x': x, 'L0_tok_w': _L0_tok_in['w'], 'L0_attn_w_qkv': _L0_attn_in['w_qkv'], 'L0_attn_b_qkv': _L0_attn_in['b_qkv'], 'L0_attn_w_proj': _L0_attn_in['w_proj'], 'L0_attn_b_proj': _L0_attn_in['b_proj'], 'L0_attn_sw_qkv': _L0_attn_in['sw_qkv'], 'L0_attn_sw_proj': _L0_attn_in['sw_proj'], 'L0_attn_s_a1': _L0_attn_in['s_a1'], 'L0_attn_s_attn': _L0_attn_in['s_attn'], 'L0_attn_s_a2': _L0_attn_in['s_a2'], 'L0_attn_s_a3': _L0_attn_in['s_a3'], 'L0_ffn_scale': _L0_ffn_in['scale'], 'L0_ffn_gate_w': _L0_ffn_in['gate_w'], 'L0_ffn_gate_b': _L0_ffn_in['gate_b'], 'L0_ffn_w1': _L0_ffn_in['w1'], 'L0_ffn_b1': _L0_ffn_in['b1'], 'L0_ffn_w2': _L0_ffn_in['w2'], 'L0_ffn_b2': _L0_ffn_in['b2']}

def reference(x, L0_tok_w, L0_attn_w_qkv, L0_attn_b_qkv, L0_attn_w_proj, L0_attn_b_proj, L0_attn_sw_qkv, L0_attn_sw_proj, L0_attn_s_a1, L0_attn_s_attn, L0_attn_s_a2, L0_attn_s_a3, L0_ffn_scale, L0_ffn_gate_w, L0_ffn_gate_b, L0_ffn_w1, L0_ffn_b1, L0_ffn_w2, L0_ffn_b2):
    import jax
    import jax.numpy as jnp

    def _L0_tok_ref(x, w):
        import jax, jax.numpy as jnp
        import numpy as np
        POOL_SIZE = 2
        STRIDE = 2
        CHANNELS = 192
        B, S, C = x.shape
        n_windows = (S - POOL_SIZE) // STRIDE + 1
        window = jnp.stack([x[:, i::STRIDE, :][:, :n_windows, :] for i in range(POOL_SIZE)], axis=2)
        scores = jnp.einsum('bnpc,cd->bnpd', window, w)
        weights = jax.nn.softmax(scores, axis=2)
        return jnp.sum(weights * window, axis=2)

    def _L0_attn_ref(x, w_qkv, b_qkv, w_proj, b_proj, sw_qkv, sw_proj, s_a1, s_attn, s_a2, s_a3):
        import jax, jax.numpy as jnp
        import numpy as np
        NUM_HEADS = 12
        S_BITS = 4
        ZP = 128.0

        def fq_act(t, s):
            q = jnp.clip(jnp.round(t / s) + ZP, 0.0, 255.0)
            return (q - ZP) * s

        def fq_weight(w, s):
            sc = s[:, None]
            return jnp.clip(jnp.round(w / sc), -128.0, 127.0) * sc

        def log_int_softmax(x, scale, bits=S_BITS):
            x_int = x / scale
            x_int = x_int - jnp.max(x_int, axis=-1, keepdims=True)
            n = 30.0
            x0_int = jnp.floor(-0.6931 / scale)
            x_int = jnp.maximum(x_int, n * x0_int)
            q = jnp.floor(x_int / x0_int)
            r = x_int - x0_int * q
            c0 = 0.35815147
            b_int = jnp.floor(0.96963238 / c0 / scale)
            c_int = jnp.floor(1.0 / c0 / (scale * scale))
            z = r * (r + b_int) + c_int
            exp_int = jnp.maximum(jnp.floor(z * jnp.exp2(n - q)), 0.0)
            exp_sum = jnp.sum(exp_int, axis=-1, keepdims=True)
            ratio = jnp.round(exp_sum / jnp.maximum(exp_int, 1.0))
            big = jnp.floor(jnp.log2(ratio))
            big = big + jnp.where(ratio - jnp.exp2(big) >= jnp.exp2(big - 1.0), 1.0, 0.0)
            qmax = 2.0 ** bits
            out = jnp.exp2(-jnp.clip(big, 0.0, qmax - 1.0))
            return jnp.where((big >= qmax) | (exp_int == 0.0), 0.0, out)
        B, N, C = x.shape
        H = NUM_HEADS
        Dh = C // H
        h = x @ fq_weight(w_qkv, sw_qkv).T + b_qkv
        h = fq_act(h, s_a1)
        qkv = h.reshape(B, N, 3, H, Dh).transpose(2, 0, 3, 1, 4)
        q, k, v = (qkv[0], qkv[1], qkv[2])
        attn = jnp.einsum('bhnd,bhmd->bhnm', q, k) * Dh ** (-0.5)
        attn = fq_act(attn, s_attn)
        attn = log_int_softmax(attn, s_attn)
        o = jnp.einsum('bhnm,bhmd->bhnd', attn, v)
        o = o.transpose(0, 2, 1, 3).reshape(B, N, C)
        o = fq_act(o, s_a2)
        o = o @ fq_weight(w_proj, sw_proj).T + b_proj
        return fq_act(o, s_a3)

    def _L0_ffn_ref(x, scale, gate_w, gate_b, w1, b1, w2, b2):
        import jax, jax.numpy as jnp
        import numpy as np
        B, S, H = (2, 256, 192)
        E, K, I = (16, 4, 192)
        ALPHA, LIMIT, EPS = (1.702, 7.0, 1e-05)

        def _swiglu(h):
            x_glu, x_lin = jnp.split(h, 2, axis=-1)
            x_glu = jnp.minimum(x_glu, LIMIT)
            x_lin = jnp.clip(x_lin, -LIMIT, LIMIT)
            return x_glu * jax.nn.sigmoid(ALPHA * x_glu) * (x_lin + 1.0)
        Bx, Sx, Hx = x.shape
        xf = x.astype(jnp.float32)
        t = xf * jax.lax.rsqrt(jnp.mean(xf * xf, axis=-1, keepdims=True) + EPS) * scale
        t = t.reshape(-1, Hx)
        T = t.shape[0]
        g = t @ gate_w.T + gate_b
        vals, idx = jax.lax.top_k(g, K)
        w = jax.nn.softmax(vals, axis=-1) / K
        full_w = jnp.zeros((T, E), jnp.float32).at[jnp.arange(T)[:, None], idx].set(w)
        h = jnp.einsum('th,ehf->tef', t, w1) + b1
        h = _swiglu(h)
        y = jnp.einsum('tei,eih->teh', h, w2) + b2
        out = jnp.einsum('teh,te->th', y, full_w) * K
        return x + out.astype(x.dtype).reshape(Bx, Sx, Hx)
    h = _L0_tok_ref(x, L0_tok_w)
    h = h + _L0_attn_ref(_layernorm(h, axis=-1), L0_attn_w_qkv, L0_attn_b_qkv, L0_attn_w_proj, L0_attn_b_proj, L0_attn_sw_qkv, L0_attn_sw_proj, L0_attn_s_a1, L0_attn_s_attn, L0_attn_s_a2, L0_attn_s_a3)
    h = h + _L0_ffn_ref(_layernorm(h, axis=-1), L0_ffn_scale, L0_ffn_gate_w, L0_ffn_gate_b, L0_ffn_w1, L0_ffn_b1, L0_ffn_w2, L0_ffn_b2)
    return h

_drawn_inputs = setup_inputs


def setup_inputs(seed=0):
    import zlib

    import numpy as np

    out = dict(_drawn_inputs(seed))
    spreads = {'L0_ffn_scale': (1.0, 0.6), 'L0_ffn_gate_b': (0.0, 0.8)}
    factors = {'L0_attn_w_qkv': 6.823,
     'L0_attn_b_qkv': 7.768,
     'L0_attn_w_proj': 4.969,
     'L0_attn_sw_qkv': 8.0,
     'L0_attn_sw_proj': 51.679,
     'L0_ffn_gate_w': 5.22,
     'L0_ffn_w1': 4.879,
     'L0_ffn_b1': 8.0,
     'L0_ffn_w2': 4.775,
     'L0_ffn_b2': 8.0}
    for name, (base, spread) in spreads.items():
        noise = np.random.default_rng([zlib.crc32(name.encode()), seed]).standard_normal(out[name].shape)
        drawn = base * np.exp(spread * noise) if base else spread * noise
        out[name] = jnp.asarray(drawn.astype(out[name].dtype))
    for name, factor in factors.items():
        out[name] = (out[name] * factor).astype(out[name].dtype)
    return out
```

```python
from contextlib import ExitStack

import concourse.bass as bass
import numpy as np
from concourse import mybir

BATCH, SEQ, C = 64, 375, 192
TOK = (SEQ - 2) // 2 + 1
REST = TOK - 128
BLOCKS = BATCH // 2
HEADS, DH = 12, 16
EXPERTS, TOPK = 16, 4
PAD = 64 - REST
REST_ROWS = ((0, REST), (64 + PAD, 128))
COLS = 384
SLOT_COL = (0, 256, 128)
KEY_COL = (0, 192 + PAD)
TILES = EXPERTS * 3 // 2
STEPS = 24
GROUPS, GH = 3, 4
UNITS = 3 * GH
UW = TOK
GW = UNITS * UW
W1COLS = TILES * 256 + EXPERTS
WSCALE = 64.0
MAGIC = 1.5 * 2.0**23
HMAGIC = 1536.0
BIG = 3.0e38
LIMIT, ALPHA = 7.0, 1.702
GLU_MAX = LIMIT / (1.0 + float(np.exp(-ALPHA * LIMIT)))
EPS = 1e-5

LOOP_FROM, LOOP_TO = 4, 30
LAST_BODY = BLOCKS + 2


def build(nc, a):
    dt, ALU, ACT, AX = mybir.dt, mybir.AluOpType, mybir.ActivationFunctionType, mybir.AxisListType
    f32, f16, bf16, u16, i16 = dt.float32, dt.float16, dt.bfloat16, dt.uint16, dt.int16
    ctx = ExitStack()
    with ctx:
        def sb(name, shape, d):
            return ctx.enter_context(nc.sbuf_tensor(name, shape, d))

        class Signal:

            def __init__(self, name, per=1):
                self.sem, self.per = ctx.enter_context(nc.semaphore(name)), per

            def at(self, b, i=0):
                v = b * self.per + (i + 1)
                return (prep.sem, 1) if isinstance(v, int) and v <= 0 else (self.sem, v)

        def plain(eng):
            eng.sem_inc(taken.sem, 1)

        id16 = sb("id16", [128, 128], f16)
        id32 = sb("id32", [128, 128], f32)
        sel = sb("sel", [32, TILES * 128], f16)
        tokw = sb("tokw", [128, 2, C], f32)
        wqk = sb("wqk", [128, 2, 960], f16)
        wp = sb("wp", [128, 3, C], f16)
        w1h0 = sb("w1h0", [128, W1COLS], f16)
        w1hR = sb("w1hR", [128, W1COLS], f16)
        w1l0 = sb("w1l0", [128, W1COLS], f16)
        w1l5 = sb("w1l5", [128, W1COLS], f16)
        w2 = sb("w2", [128, TILES, C], f32)
        b2 = sb("b2", [48, C], f32)
        scal = sb("scal", [128, 4], f32)
        iscal = sb("iscal", [128, 4], f32)
        consts = sb("consts", [128, 32], f32)
        qscale = sb("qscale", [128, 6], f32)
        qbias = sb("qbias", [128, 6], f32)
        vrow = sb("vrow", [128, 2, C], f32)
        prow = sb("prow", [128, 2, C], f32)
        lnscale = sb("lnscale", [128, 2], f32)
        vmask = sb("vmask", [128, 2], f32)
        negh = sb("negh", [128, 4], f32)
        magic = sb("magic", [128, 1], f32)
        x = sb("x", [128, 3, 2 * C], f32)
        dif = sb("dif", [128, 3, C], f32)
        dT = sb("dT", [128, 2, COLS], f32)
        th = sb("th", [128, 3, C], f32)
        h1 = [sb(f"h1{i}", [128, 3, C], f32) for i in range(2)]
        hres = sb("hres", [128, 3, C], f32)
        xn = th
        split = sb("split", [128, 3, 2 * C], f16)
        hi, lo_rest, lo_main = split[:, :, 0:C], split[:, :, C:256], split[:, :, 256:384]
        xT = sb("xT", [128, 3, COLS], f16)
        stats = sb("stats", [128, 3, 8], f32)
        mv = sb("mv", [128, 3, 2], f32)
        vare = sb("vare", [128, 4], f32)
        rstd = sb("rstd", [128, 4], f32)
        qf = sb("qf", [128, COLS], f32)
        qr = sb("qr", [128, COLS], f16)
        qT = [sb(f"qT{i}", [128, 3, COLS], f16) for i in range(2)]
        kT = [sb(f"kT{i}", [128, 3, COLS], f16) for i in range(2)]
        vt = [sb(f"vt{i}", [128, 4, HEADS, 32], bf16) for i in range(2)]
        y = sb("y", [128, UNITS, UW], f32)
        flat16 = [sb(n, [128, GW], f16) for n in ("ai", "q1", "xq")]
        ai, q1, xq = (v[:].rearrange("p (u n) -> p u n", u=UNITS) for v in flat16)
        ee = sb("ee", [128, UNITS, UW], f32)
        f4 = q1[:].bitcast(u16)
        pat = sb("pat", [128, GW + 12], i16)
        rmax = sb("rmax", [128, UNITS], f32)
        rsum = sb("rsum", [128, UNITS], f32)
        rs4 = sb("rs4", [128, UNITS], f32)
        pt = [sb(f"pt{i}", [128, 288], f32) for i in range(2)]
        of = sb("of", [128, COLS], f32)
        orr = sb("orr", [128, COLS], f16)
        oT = sb("oT", [128, GROUPS, COLS], f16)
        pf = sb("pf", [128, 3, C], f32)
        vf = pf
        h2 = sb("h2", [128, 3, C], f32)
        cn = sb("cn", [128, 3, C], f32)
        ct = pf
        cstats = sb("cstats", [128, 3, 8], f32)
        cmv = sb("cmv", [128, 3, 2], f32)
        cvar = sb("cvar", [128, 4], f32)
        crstd = sb("crstd", [128, 4], f32)
        cvar2 = sb("cvar2", [128, 4], f32)
        crstd2 = sb("crstd2", [128, 4], f32)
        res = [sb(f"res{i}", [128, 3, C], f32) for i in range(2)]
        tT = [sb(f"tT{i}", [128, 4, COLS], f16) for i in range(2)]
        g20 = sb("g20", [128, 3, 20], f32)
        gz = sb("gz", [128, 3, 20], f32)
        top8 = sb("top8", [128, 3, 8], f32)
        rep8 = sb("rep8", [128, 3, 8], f32)
        gm = sb("gm", [128, 3, EXPERTS], f32)
        gd = sb("gd", [128, 3, EXPERTS], f32)
        gt = sb("gt", [128, 3, EXPERTS], f32)
        gn = sb("gn", [128, 3, EXPERTS], f32)
        gr = sb("gr", [128, 3, EXPERTS], f32)
        gs = sb("gs", [128, 4], f32)
        gsr = sb("gsr", [128, 4], f32)
        gw = sb("gw", [128, 3, 48], f32)
        gh16 = sb("gh16", [128, 3, EXPERTS], f16)
        wT32 = [sb(f"wT32{i}", [48, COLS], f32) for i in range(2)]
        wT16 = [w[0:32, 0:COLS // 2].bitcast(f16) for w in wT32]
        u = [sb(f"u{i}", [128, COLS], f32) for i in range(2)]
        lc = [sb(f"lc{i}", [128, COLS], f32) for i in range(2)]
        p = [sb(f"p{i}", [128, COLS], f32) for i in range(2)]
        act = [sb(f"act{i}", [128, COLS], f32) for i in range(4)]
        yo = sb("yo", [128, 3, C], f32)
        wst = y[:].rearrange("p u n -> p (u n)")[:, 0:1536].rearrange("p (t f) -> p t f", t=2)
        wtmp = [v[:].bitcast(f32) for v in flat16[1:]]
        bst = ee[:].rearrange("p u n -> p (u n)")[:, 0:768]
        bs = ee[:].rearrange("p u n -> p (u n)")[:, 1408:2176]
        bh = ee[:].rearrange("p u n -> p (u n)")[:, 1024:1408].bitcast(f16)

        bank = [ctx.enter_context(nc.psum_tensor(f"bank{i}", [128, 512], f32)) for i in range(8)]
        B_SC, B_PT, B_AV, B_Y1, B_G, B_L, B_W, B_Y0 = bank

        ld_const = Signal("ld_const")
        x_loaded = Signal("x_loaded")
        w_loaded = Signal("w_loaded")
        stored = Signal("stored")
        prep = Signal("prep")
        prep_act = Signal("prep_act")
        w_ready = Signal("w_ready")
        w_high = Signal("w_high")
        w_split = Signal("w_split")
        a_keep = Signal("a_keep")
        taken = Signal("taken")
        a_dif = Signal("a_dif")
        a_difT_ps = Signal("a_difT_ps", 2)
        a_difT = Signal("a_difT", 2)
        a_sc_ps = Signal("a_sc_ps", 2)
        a_tanh = Signal("a_tanh", 2)
        a_dve = Signal("a_dve", 6)
        a_rstd = Signal("a_rstd")
        a_split = Signal("a_split", 2)
        a_xT_ps = Signal("a_xT_ps", 2)
        a_xT = Signal("a_xT", 2)
        a_qk_ps = Signal("a_qk_ps", 6)
        a_qk_lin = Signal("a_qk_lin", 6)
        a_qk_rnd = Signal("a_qk_rnd", 6)
        a_qk = Signal("a_qk", 6)
        a_v_ps = Signal("a_v_ps", 2)
        a_v_dve = Signal("a_v_dve", 10)
        b_sc_ps = Signal("b_sc_ps", 24)
        b_y = Signal("b_y", 24)
        b_dve = Signal("b_dve", 3 * 18)
        b_sq = Signal("b_sq", 3)
        b_t4 = Signal("b_t4", 3)
        v_pt_ps = Signal("v_pt_ps", 12)
        v_pt = Signal("v_pt", 12)
        v_av_ps = Signal("v_av_ps", 12)
        v_lin = Signal("v_lin", 3)
        v_rnd = Signal("v_rnd", 3)
        v_o = Signal("v_o", 3)
        c_proj_ps = Signal("c_proj_ps", 2)
        c_dve = Signal("c_dve", 40)
        c_rstd = Signal("c_rstd", 2)
        c_tT_ps = Signal("c_tT_ps", 2)
        c_tT = Signal("c_tT", 3)
        c_gate_ps = Signal("c_gate_ps")
        c_tanh = Signal("c_tanh")
        c_wT_ps = Signal("c_wT_ps")
        c_wT = Signal("c_wT", 2)
        d_g_ps = Signal("d_g_ps", TILES)
        d_l_ps = Signal("d_l_ps", TILES)
        d_w_ps = Signal("d_w_ps", TILES)
        d_u = Signal("d_u", TILES)
        d_lc = Signal("d_lc", TILES)
        d_p = Signal("d_p", TILES)
        d_act = Signal("d_act", TILES)
        d_y_ps = Signal("d_y_ps", TILES)
        d_out = Signal("d_out", 2)

        KAPPA, KX, NINVX, Q1OFF, CLAMP, HB, CP, KO, KP3, S3C = range(10)

        def cc(i):
            return consts[:, i:i + 1]

        def runs_a(k):
            return not isinstance(k, int) or 0 <= k + 1 < BLOCKS

        def runs(b):
            return not isinstance(b, int) or 0 <= b < BLOCKS

        def slot_cols(t2d, s):
            return t2d[:, SLOT_COL[s]:SLOT_COL[s] + 128]

        A_HD, A_H, A_STAT, A_AGG, A_VAR, A_XN = range(6)
        (B_CLIP, B_MAX, B_MCLIP, B_SUB, B_CLAMP, B_Q1, B_XQ, B_P2, B_R, B_E, B_S, B_S4, B_RS4, B_F4, B_T6,
         B_MASK, B_PAT) = range(17)
        NB = 18
        (C_PROJ0, C_PROJ1, C_BIAS, C_RND, C_CLIP, C_H2, C_STAT, C_AGG, C_VAR, C_V1, C_V2, C_XN, C_T, C_HI, C_LO,
         C_RES, C_GATE, C_TOP, C_REP, C_MR, C_MASK, C_D, C_NUM, C_DEN, C_RCP, C_E1, C_E2, C_SUM, C_SR, C_W,
         C_H16, C_HI32, C_LO32) = range(33)
        NC_ = 40

        def b_steps(k, t):
            g, s = t // 8 - 1, t % 8
            b = k
            if g < 0:
                b, g = k - 1, GROUPS - 1
            return [(b, g, s)] if runs(b) else []

        def v_steps(k, t):
            if t < 0:
                return []
            b, g, i = {0: (k - 1, 1, t), 1: (k - 1, 2, t - 8), 2: (k, 0, t - 16)}[t // 8]
            return [(b, g, i)] if i < GH and runs(b) else []

        PREP_DONE = 44
        block = ctx.enter_context(nc.Block())

        def bodies(eng, body):
            for k in range(-1, LOOP_FROM):
                body(k, k % 2)
            with eng.Fori(0, (LOOP_TO - LOOP_FROM) // 2) as turn:
                body(turn * 2 + LOOP_FROM, 0)
                body(turn * 2 + (LOOP_FROM + 1), 1)
            for k in range(LOOP_TO, LAST_BODY + 1):
                body(k, k % 2)

        N_CONST = 19

        @block.sync
        def _(sp):
            for dst, src in [
                (id16[:], a["id16"]), (id32[:], a["id32"]), (sel[:], a["sel"]),
                (tokw[:, 0, :], a["tokw"][0:128, :]), (tokw[0:64, 1, :], a["tokw"][128:192, :]),
                (scal[:], a["scal"].to_broadcast([128, 4])),
                (qscale[:], a["sw_col"]), (qbias[:], a["b_col"]),
                (y[:].rearrange("p u n -> p (u n)")[:, 0:1920].rearrange("p (t f) -> p t f", t=2), a["wqk"]),
                (flat16[0][:].bitcast(f32)[:, 0:960], a["sw_row"].to_broadcast([128, 960])),
                (vrow[:, 0, :], a["sw_row"][:, 768:960].to_broadcast([128, C])),
                (vrow[:, 1, :], a["bv_row"].to_broadcast([128, C])),
                (ee[:].rearrange("p u n -> p (u n)")[:, 0:576].rearrange("p (t f) -> p t f", t=3), a["wp"]),
                (prow[:, 0, :], a["sp_row"].to_broadcast([128, C])),
                (prow[:, 1, :], a["bp_row"].to_broadcast([128, C])),
                (lnscale[:], a["lnscale"]), (vmask[:], a["vmask"]), (b2[32:48, :], a["b2"]), (w2[:, :, :], a["w2"]),
                            ]:
                sp.dma_start(dst, src).then_inc(ld_const.sem, 16)

            def load_x(b):
                sp.wait_ge(*a_dve.at(b - 1, A_H))
                for i in range(2):
                    row = a["x"][b * 2 + i, :]
                    sp.dma_start(x[:, i, :], row[0:128 * 2 * C].rearrange("(n f) -> n f", f=2 * C)
                                 ).then_inc(x_loaded.sem, 16)
                    sp.dma_start(x[REST_ROWS[i][0]:REST_ROWS[i][1], 2, :],
                                 row[128 * 2 * C:TOK * 2 * C].rearrange("(n f) -> n f", f=2 * C)
                                 ).then_inc(x_loaded.sem, 16)

            def store(b):
                sp.wait_ge(*d_out.at(b, 1))
                for i in range(2):
                    sp.dma_start(a["out"][b * 2 + i, 0:128, :], yo[:, i, :]).then_inc(stored.sem, 16)
                    sp.dma_start(a["out"][b * 2 + i, 128:TOK, :], yo[REST_ROWS[i][0]:REST_ROWS[i][1], 2, :]
                                 ).then_inc(stored.sem, 16)

            sp.wait_ge(prep.sem, 1)
            load_x(0)

            def body(k, par):
                if isinstance(k, int) and k == 0:
                    sp.wait_ge(prep.sem, PREP_DONE)
                    for c in range(9):
                        if c:
                            sp.wait_ge(w_ready.sem, c)
                        n = 768 if c < 8 else EXPERTS
                        sp.dma_start(wst[:, :, 0:n], a["w1"][:, :, 768 * c:768 * c + n]).then_inc(w_loaded.sem, 16)
                        for r in (64, 96):
                            sp.dma_start(bst[r:r + 1, 0:n], a["b1"][:, 768 * c:768 * c + n]).then_inc(w_loaded.sem, 16)
                if runs(k + 2):
                    load_x(k + 2)
                if runs(k - 3):
                    store(k - 3)

            bodies(sp, body)
            sp.wait_ge(stored.sem, 64 * BLOCKS)

        def misc_jobs(k, t):
            jobs = []
            if runs(k + 1):
                A = {0: ("difT0", a_difT, 0), 1: ("difT1", a_difT, 1), 3: ("sc0", a_tanh, 0), 4: ("sc1", a_tanh, 1),
                     9: ("xT0", a_xT, 0), 10: ("xT1", a_xT, 1), 11: ("qk0", a_qk_lin, 0), 12: ("qk1", a_qk_lin, 1),
                     13: ("qk2", a_qk_lin, 2), 16: ("qk3", a_qk_lin, 3)}
                if t in A:
                    jobs.append((A[t][0], k + 1, A[t][1], A[t][2]))
            if runs(k):
                A2 = {2: ("v0", a_v_dve, 0), 5: ("v1", a_v_dve, 5), 6: ("qk4", a_qk_lin, 4), 7: ("qk5", a_qk_lin, 5)}
                if t in A2:
                    jobs.append((A2[t][0], k, A2[t][1], A2[t][2]))
            if runs(k - 1):
                Cs = {14: ("pr0", c_dve, C_PROJ0), 15: ("pr1", c_dve, C_PROJ1), 18: ("tT0", c_tT, 0),
                      19: ("tT1", c_tT, 2), 20: ("gate", c_dve, C_GATE), 22: ("wT", c_wT, 1)}
                if t in Cs:
                    jobs.append((Cs[t][0], k - 1, Cs[t][1], Cs[t][2]))
            return jobs

        @block.tensor
        def _(pe):
            mm = nc.tensor.matmul
            last_reader = [None]

            def claim_w(k):
                if last_reader[0] is not None:
                    sig, off, i = last_reader[0]
                    pe.wait_ge(*sig.at(k + off, i))

            def misc(k, par, name, b, bpar):
                if name in ("difT0", "difT1"):
                    if name == "difT0":
                        pe.wait_ge(*a_dif.at(b))
                    for s in range(3):
                        c0, n = (0, 128) if name == "difT0" else (128, 64)
                        out = slot_cols(B_W[0:n, 0:COLS], s)
                        last = nc.tensor.transpose(out, dif[:, s, c0:c0 + n], id32[:])
                    last.then_inc(a_difT_ps.sem, 1)
                elif name in ("sc0", "sc1"):
                    pe.wait_ge(*a_difT.at(b, 1))
                    for s in ((0, 1) if name == "sc0" else (2,)):
                        o = B_W[:, 192 * (s % 2):192 * (s % 2) + 192]
                        mm(o, slot_cols(dT[:, 0, :], s), tokw[:, 0, :], start=True, stop=False)
                        last = mm(o, slot_cols(dT[0:64, 1, :], s), tokw[0:64, 1, :], start=False, stop=True)
                    last.then_inc(a_sc_ps.sem, 1)
                elif name in ("xT0", "xT1", "tT0", "tT1"):
                    A = name[0] == "x"
                    pe.wait_ge(*(a_split.at(b, 1) if A else c_dve.at(b, C_LO)))
                    ps = B_W[:].bitcast(f16)
                    for s in range(3):
                        if name[2] == "0":
                            nc.tensor.transpose(slot_cols(ps[:, 0:COLS], s), split[:, s, 0:128], id16[:])
                            last = nc.tensor.transpose(slot_cols(ps[:, COLS:2 * COLS], s), lo_main[:, s, :], id16[:])
                        else:
                            last = nc.tensor.transpose(slot_cols(ps[:, 0:COLS], s), split[:, s, 128:256], id16[:])
                    last.then_inc((a_xT_ps if A else c_tT_ps).sem, 1)
                elif name[:2] == "qk":
                    i = int(name[2])
                    pe.wait_ge(*a_xT.at(b, 1))
                    f0 = (i % 2) * 384 + (i // 2) * 128
                    for j in range(3):
                        last = mm(B_W[:, 0:COLS], wqk[:, j // 2, f0:f0 + 128], xT[:, j, :], start=j == 0, stop=j == 2)
                    last.then_inc(a_qk_ps.sem, 1)
                elif name in ("v0", "v1"):
                    for s in ((0, 1) if name == "v0" else (2,)):
                        o = B_W[:, 192 * (s % 2):192 * (s % 2) + 192]
                        for j in range(3):
                            last = mm(o, slot_cols(xT[:, j, :], s), wqk[:, j // 2, 768:960], start=j == 0, stop=j == 2)
                    last.then_inc(a_v_ps.sem, 1)
                elif name in ("pr0", "pr1"):
                    pe.wait_ge(*v_o.at(b, 2))
                    for s in ((0, 1) if name == "pr0" else (2,)):
                        o = B_W[:, 192 * (s % 2):192 * (s % 2) + 192]
                        for j in range(GROUPS):
                            last = mm(o, slot_cols(oT[:, j, :], s), wp[:, j, :], start=j == 0, stop=j == 2)
                    last.then_inc(c_proj_ps.sem, 1)
                elif name == "gate":
                    pe.wait_ge(*c_tT.at(b, 2))
                    t_ = tT[bpar]
                    g0 = TILES * 256
                    for s in range(3):
                        for n, (j, w) in enumerate([(0, w1h0), (1, w1h0), (2, w1hR), (0, w1l0), (3, w1l5)]):
                            last = mm(B_W[:, 16 * s:16 * s + 16], slot_cols(t_[:, j, :], s), w[:, g0:g0 + EXPERTS],
                                      start=n == 0, stop=n == 4)
                    last.then_inc(c_gate_ps.sem, 1)
                elif name == "wT":
                    pe.wait_ge(*c_dve.at(b, C_LO32))
                    plain(pe)
                    for s in range(3):
                        last = nc.tensor.transpose(slot_cols(B_W[0:48, 0:COLS], s), gw[:, s, :], id32[:])
                    last.then_inc(c_wT_ps.sem, 1)

            def body(k, par):
                d, dp = k - 2, par
                for t in range(STEPS):
                    on_d = runs(d)
                    if on_d:
                        if t == 0:
                            pe.wait_ge(*c_tT.at(d, 2))
                            pe.wait_ge(*c_wT.at(d, 1))
                            if isinstance(k, int) and k == 2:
                                pe.wait_ge(w_ready.sem, 9)
                        T = tT[dp]
                        c0 = 768 * (t // 3) + 128 * (t % 3)

                        def products(ps, col):
                            for n, (j, w) in enumerate([(0, w1h0), (1, w1h0), (2, w1hR), (0, w1l0), (3, w1l5)]):
                                last = mm(ps[:, 0:COLS], w[:, col:col + 128], T[:, j, :], start=n == 0, stop=n == 4)
                            return last
                        pe.wait_ge(*d_u.at(d, t - 1))
                        products(B_G, c0).then_inc(d_g_ps.sem, 1)
                    for name, b, sig, i in misc_jobs(k, t):
                        claim_w(k)
                        if name == "difT1":
                            plain(pe)
                        off = 1 if name in ("difT0", "difT1", "sc0", "sc1", "xT0", "xT1", "qk0", "qk1", "qk2", "qk3") else (
                            0 if name in ("v0", "v1", "qk4", "qk5") else -1)
                        misc(k, par, name, b, (par + off) % 2)
                        last_reader[0] = (sig, off, i)
                    if on_d:
                        pe.wait_ge(*d_lc.at(d, t - 1))
                        products(B_L, c0 + 384).then_inc(d_l_ps.sem, 1)
                    b3, t3 = (d, t - 3) if t >= 3 else (d - 1, t + 21)
                    if runs(b3):
                        if t3 == 0:
                            pe.wait_ge(*d_out.at(b3 - 1, 1))
                            for s in range(3):
                                o = (B_Y0, B_Y1)[s // 2][:, 192 * (s % 2):192 * (s % 2) + 192]
                                mm(o, slot_cols(wT32[b3 % 2 if isinstance(b3, int) else dp][32:48, :], s), b2[32:48, :],
                                   start=s != 1, stop=False, skip_group_check=True)
                        pe.wait_ge(*d_act.at(b3, t3))
                        for s in range(3):
                            o = (B_Y0, B_Y1)[s // 2][:, 192 * (s % 2):192 * (s % 2) + 192]
                            last = mm(o, slot_cols(act[t3 % 4][:, :], s), w2[:, t3, :], start=False,
                                      stop=t3 == TILES - 1, skip_group_check=True)
                        last.then_inc(d_y_ps.sem, 1)
                    if on_d:
                        claim_w(k)
                        mm(B_W[:, 0:COLS], sel[:, 128 * t:128 * t + 128], wT16[dp], start=True, stop=True
                           ).then_inc(d_w_ps.sem, 1)
                        last_reader[0] = (d_p, -2, t)
                    if runs(k):
                        h = t // 2
                        r0 = 32 * (h % 4)
                        Q, K = qT[par][r0:r0 + DH, h // 4, :], kT[par][r0:r0 + DH, h // 4, :]
                        pe.wait_ge(*a_qk.at(k, 2 * (h // 4) + 1))
                        pe.wait_ge(*b_y.at(k, t - 1))
                        if t % 2 == 0:
                            for b in range(2):
                                last = mm(B_SC[:, UW * b:UW * b + UW], Q[:, 256 * b:256 * b + 128],
                                          K[:, KEY_COL[b]:KEY_COL[b] + UW], start=True, stop=True)
                        else:
                            for b in range(2):
                                last = mm(B_SC[64 * b:64 * b + 64, 0:UW], Q[:, 128 + 64 * b:192 + 64 * b],
                                          K[:, KEY_COL[b]:KEY_COL[b] + UW], start=True, stop=True)
                        last.then_inc(b_sc_ps.sem, 1)
                    for bv, g, i in v_steps(k, t - 1):
                        vp = (par + (0 if t > 15 else 1)) % 2
                        V = vt[vp]
                        P = pt[i % 2][:].bitcast(bf16)
                        if i == 0:
                            pe.wait_ge(*v_lin.at(bv, g - 1))
                            pe.wait_ge(*a_v_dve.at(bv, 9))
                        pe.wait_ge(*v_pt.at(bv, 4 * g + i))
                        for b in range(2):
                            o = B_AV[32 * i:32 * i + 32, 192 * b:192 * b + 192]
                            mm(o, V[:, b, 4 * g + i, :], P[:, 192 * b:192 * b + 192], start=True, stop=False)
                            last = mm(o, V[:, 2 + b, 4 * g + i, :], P[:, 384:576],
                                      start=False, stop=True)
                        last.then_inc(v_av_ps.sem, 1)
                    for bv, g, i in v_steps(k, t):
                        pp = pat
                        ps = B_PT[:].bitcast(f16)
                        src = pp[:].bitcast(f16)
                        pe.wait_ge(*b_dve.at(bv, NB * g + B_PAT))
                        pe.wait_ge(*v_pt.at(bv, 4 * g + i - 1))
                        main, rest = (0, REST), (128, -PAD)
                        for n in range(2):
                            w0, q0 = (3 * i + n) * UW, 384 + 64 * n
                            nc.tensor.transpose(ps[:, 256 * n:256 * n + 128], src[:, w0 + main[n]:w0 + main[n] + 128],
                                                id16[:])
                            nc.tensor.transpose(ps[64 * n:64 * n + 64, q0:q0 + 128],
                                                src[:, w0 + rest[n]:w0 + rest[n] + 64], id16[:])
                        w0 = (3 * i + 2) * UW
                        nc.tensor.transpose(ps[:, 128:256], src[:, w0 + main[1]:w0 + main[1] + 128], id16[:])
                        nc.tensor.transpose(ps[:, 128:192], src[0:64, w0 + main[0]:w0 + main[0] + 128],
                                            id16[0:64, 0:64])
                        for n in range(2):
                            rows, q0 = slice(64 * n, 64 * n + 64), 512 - 128 * n
                            last = nc.tensor.transpose(ps[rows, q0:q0 + 64], src[rows, w0 + rest[n]:w0 + rest[n] + 64],
                                                       id16[rows, rows])
                        last.then_inc(v_pt_ps.sem, 1)
                if last_reader[0] is not None:
                    sig, off, i = last_reader[0]
                    last_reader[0] = (sig, off - 1, i)

            pe.wait_ge(prep.sem, PREP_DONE)
            pe.wait_ge(prep_act.sem, 1)
            bodies(pe, body)

        @block.scalar
        def _(sc):
            S = nc.scalar

            def body(k, par):
                d, dp = k - 2, par
                for t in range(STEPS):
                    if runs(d):
                        sc.wait_ge(*d_g_ps.at(d, t))
                        sc.wait_ge(*d_p.at(d, t - 2))
                        S.activation(u[t % 2][:], B_G[:, 0:COLS], ACT.Gelu_apprx_sigmoid, scale=1.0 / WSCALE
                                     ).then_inc(d_u.sem, 1)
                    for name, b, _, _ in misc_jobs(k, t):
                        if name == "difT0":
                            sc.wait_ge(*a_difT_ps.at(b, 0))
                            sc.wait_ge(*a_sc_ps.at(b - 1, 1))
                            S.copy(dT[:, 0, :], B_W[:, 0:COLS]).then_inc(a_difT.sem, 1)
                        elif name == "difT1":
                            sc.wait_ge(*a_difT_ps.at(b, 1))
                            S.copy(dT[0:64, 1, :], B_W[0:64, 0:COLS]).then_inc(a_difT.sem, 1)
                        elif name in ("sc0", "sc1"):
                            i = int(name[2])
                            sc.wait_ge(*a_sc_ps.at(b, i))
                            sc.wait_ge(*a_dve.at(b - 1, A_HD))
                            n = 2 - i
                            S.activation(th[:, 2 * i:2 * i + n, :],
                                         B_W[:, 0:192 * n].rearrange("p (s c) -> p s c", s=n), ACT.Tanh, scale=0.5
                                         ).then_inc(a_tanh.sem, 1)
                        elif name in ("xT0", "xT1"):
                            i = int(name[2])
                            sc.wait_ge(*a_xT_ps.at(b, i))
                            if i == 0:
                                sc.wait_ge(*a_qk_ps.at(b - 1, 5))
                            n = 2 - i
                            S.copy(xT[:, 2 * i:2 * i + n, :].bitcast(f32), B_W[:, 0:192 * n].rearrange(
                                "p (s c) -> p s c", s=n)).then_inc(a_xT.sem, 1)
                        elif name[:2] == "qk":
                            i = int(name[2])
                            sc.wait_ge(*a_qk_ps.at(b, i))
                            sc.wait_ge(*a_qk_rnd.at(b, i - 1))
                            c = (i % 2) * 3 + i // 2
                            S.activation(qf[:], B_W[:, 0:COLS], ACT.Identity, scale=qscale[:, c:c + 1],
                                         bias=qbias[:, c:c + 1]).then_inc(a_qk_lin.sem, 1)
                        elif name == "tT0":
                            sc.wait_ge(*c_tT_ps.at(b, 0))
                            cp = (par + 1) % 2
                            S.copy(tT[cp][:, 0:2, :].bitcast(f32), B_W[:, 0:384].rearrange("p (s c) -> p s c", s=2)
                                   ).then_inc(c_tT.sem, 1)
                        elif name == "tT1":
                            sc.wait_ge(*c_tT_ps.at(b, 1))
                            cp = (par + 1) % 2
                            S.copy(tT[cp][:, 2, :].bitcast(f32), B_W[:, 0:192]).then_inc(c_tT.sem, 1)
                            S.copy(tT[cp][0:64, 3, :].bitcast(f32), B_W[0:64, 0:192]).then_inc(c_tT.sem, 1)
                        elif name == "wT":
                            sc.wait_ge(*c_wT_ps.at(b))
                            cp = (par + 1) % 2
                            S.copy(wT16[cp], B_W[0:32, 0:COLS]).then_inc(c_wT.sem, 1)
                            S.copy(wT32[cp][32:48, :], B_W[32:48, 0:COLS]).then_inc(c_wT.sem, 1)
                    if t == 3 and runs(k - 1):
                        sc.wait_ge(*a_dve.at(k - 1, A_H))
                        sc.wait_ge(*c_dve.at(k - 2, C_H2))
                        S.copy(hres[:], h1[(par + 1) % 2][:]).then_inc(a_keep.sem, 1)
                    if t == 21 and runs(k - 1):
                        sc.wait_ge(*c_dve.at(k - 1, C_D))
                        S.activation(gt[:], gd[:], ACT.Tanh, scale=0.5).then_inc(c_tanh.sem, 1)
                    for b, g, s in b_steps(k, t):
                        if s == 3:
                            sc.wait_ge(*b_dve.at(b, NB * g + B_R))
                            S.activation(ee[:], xq[:], ACT.Square, bias=cc(HB)).then_inc(b_sq.sem, 1)
                    if runs(k):
                        i = (t % 8) // 2 * 3
                        g = t // 8
                        yb = y
                        sc.wait_ge(*b_sc_ps.at(k, t))
                        if t % 8 == 0:
                            sc.wait_ge(*b_dve.at(k, NB * (g - 1) + B_CLIP))
                        if t % 2 == 0:
                            S.activation(yb[:, i:i + 2, :], B_SC[:, 0:2 * UW].rearrange("p (u n) -> p u n", u=2),
                                         ACT.Identity, scale=cc(KAPPA), bias=magic[:]).then_inc(b_y.sem, 1)
                        else:
                            S.activation(yb[:, i + 2, :], B_SC[:, 0:UW], ACT.Identity, scale=cc(KAPPA), bias=magic[:]
                                         ).then_inc(b_y.sem, 1)
                    for bv, g, i in v_steps(k, t):
                        sc.wait_ge(*v_pt_ps.at(bv, 4 * g + i))
                        sc.wait_ge(*v_av_ps.at(bv, 4 * g + i - 2))
                        S.copy(pt[i % 2][:], B_PT[:, 0:288]).then_inc(v_pt.sem, 1)
                    for bv, g, i in v_steps(k, t - 1):
                        if i == 3:
                            sc.wait_ge(*v_av_ps.at(bv, 4 * g + 3))
                            sc.wait_ge(*v_rnd.at(bv, g - 1))
                            S.activation(of[:], B_AV[:, 0:COLS], ACT.Identity, scale=cc(KO), bias=magic[:]
                                         ).then_inc(v_lin.sem, 1)

            sc.wait_ge(prep.sem, PREP_DONE)
            S.copy(consts[:, 31:32], magic[:]).then_inc(prep_act.sem, 1)

            def with_weights(k, par):
                if isinstance(k, int) and k == 0:
                    for c in range(9):
                        n = 768 if c < 8 else EXPERTS
                        sc.wait_ge(w_high.sem, c + 1)
                        S.copy(w1h0[:, 768 * c:768 * c + n], wtmp[0][:, 0:n])
                        S.copy(w1hR[:, 768 * c:768 * c + n], wtmp[1][:, 0:n]).then_inc(prep_act.sem, 1)
                body(k, par)

            bodies(sc, with_weights)

        @block.gpsimd
        def _(pool):
            G = nc.gpsimd

            def tile(b, t, par):
                pool.wait_ge(*d_p.at(b, t))
                pool.wait_ge(*d_y_ps.at(b, t - 4))
                G.tensor_tensor(act[t % 4][:], p[t % 2][:], lc[t % 2][:], ALU.mult).then_inc(d_act.sem, 1)

            def body(k, par):
                for t in range(STEPS):
                    if t == 0 and runs(k - 3):
                        tile(k - 3, TILES - 1, par)
                    if t >= 1 and runs(k - 2):
                        tile(k - 2, t - 1, par)
                    if t == 0 and runs(k + 1):
                        if not (isinstance(k, int)):
                            pool.wait_ge(x_loaded.sem, (k + 2) * 64)
                        else:
                            pool.wait_ge(x_loaded.sem, min((k + 2) * 64, 64 * BLOCKS))
                        xb = x
                        pool.wait_ge(*a_dve.at(k, A_HD))
                        pool.wait_ge(*a_difT_ps.at(k, 1))
                        G.tensor_tensor(dif[:], xb[:, :, 0:C], xb[:, :, C:2 * C], ALU.subtract).then_inc(a_dif.sem, 1)
                    if t == 7 and runs(k + 1):
                        pool.wait_ge(*a_dve.at(k + 1, A_VAR))
                        pool.wait_ge(*a_dve.at(k, A_XN))
                        G.tensor_tensor(rstd[:, 0:3], vare[:, 0:3], negh[:, 0:3], ALU.pow).then_inc(a_rstd.sem, 1)
                    if t == 16 and runs(k - 1):
                        pool.wait_ge(*c_dve.at(k - 1, C_VAR))
                        G.tensor_tensor(crstd[:, 0:3], cvar[:, 0:3], negh[:, 0:3], ALU.pow).then_inc(c_rstd.sem, 1)
                        pool.wait_ge(*c_dve.at(k - 1, C_V2))
                        G.tensor_tensor(crstd2[:, 0:3], cvar2[:, 0:3], negh[:, 0:3], ALU.pow).then_inc(c_rstd.sem, 1)
                    for b, g, s in b_steps(k, t):
                        if s in (4, 5):
                            if s == 4:
                                pool.wait_ge(*b_dve.at(b, NB * g + B_RS4))
                                plain(pool)
                            for i in range(6 * (s - 4), 6 * (s - 4) + 6):
                                last = G.tensor_scalar(ee[:, i, :], ee[:, i, :], rs4[:, i:i + 1], 1.0, ALU.mult, ALU.mult)
                            if s == 5:
                                last.then_inc(b_t4.sem, 1)

            pool.wait_ge(prep.sem, PREP_DONE)
            bodies(pool, body)

        @block.vector
        def _(ve):
            V = nc.vector
            n_prep = [0]

            def step(ins):
                n_prep[0] += 1
                ins.then_inc(prep.sem, 1)
                ve.wait_ge(prep.sem, n_prep[0])

            for tl in (x, *h1, dT, xT, qT[0], qT[1], kT[0], kT[1], vt[0], vt[1], pat, tT[0], tT[1],
                       res[0], res[1], hres, gs, vare, rstd, cvar, crstd, cvar2, crstd2):
                V.memset(tl[:], 0.0)
            step(V.memset(magic[:], MAGIC))
            for tl in (tT[0], tT[1]):
                V.memset(tl[64:65, 3, :], 1.0)
                V.memset(tl[96:97, 3, :], 1.0)
            V.memset(g20[:], BIG)
            V.memset(rep8[:], BIG)
            step(V.memset(negh[:], -0.5))
            ve.wait_ge(ld_const.sem, 16 * N_CONST)
            step(V.reciprocal(iscal[:], scal[:]))
            s1, sa, s2, s3 = (scal[:, i:i + 1] for i in range(4))
            i1, ia, i2, i3 = (iscal[:, i:i + 1] for i in range(4))
            tmp, tmq, tmr, xf0, bf_, cf = (cc(i) for i in range(10, 16))

            def ts(out, in0, sc1, sc2, op0, op1=ALU.bypass):
                if op1 == ALU.bypass:
                    return V.tensor_scalar(out, in0, sc1, None, op0)
                return V.tensor_scalar(out, in0, sc1, sc2, op0, op1)

            def floor(out, src):
                step(ts(tmq, src, MAGIC, MAGIC, ALU.add, ALU.subtract))
                step(V.tensor_tensor(tmr, tmq, src, ALU.is_gt))
                step(V.tensor_tensor(out, tmq, tmr, ALU.subtract))

            step(ts(tmp, s1, s1, 0.25, ALU.mult, ALU.mult))
            step(V.tensor_tensor(cc(KAPPA), tmp, ia, ALU.mult))
            step(ts(tmp, ia, -0.6931, None, ALU.mult))
            floor(xf0, tmp)
            step(ts(cc(KX), xf0, -1.0, None, ALU.mult))
            step(ts(cc(CLAMP), xf0, 30.0, None, ALU.mult))
            step(V.reciprocal(tmp, cc(KX)))
            step(ts(cc(NINVX), tmp, -1.0, None, ALU.mult))
            step(ts(cc(Q1OFF), tmp, 0.5, HMAGIC - 0.5, ALU.mult, ALU.add))
            step(ts(tmp, ia, 0.96963238 / 0.35815147, None, ALU.mult))
            floor(bf_, tmp)
            step(ts(tmp, ia, ia, 1.0 / 0.35815147, ALU.mult, ALU.mult))
            floor(cf, tmp)
            step(ts(cc(HB), bf_, 0.5, None, ALU.mult))
            step(V.tensor_tensor(tmp, cc(HB), cc(HB), ALU.mult))
            step(V.tensor_tensor(cc(CP), cf, tmp, ALU.subtract))
            step(ts(tmp, cf, 1.0, 2.0**47, ALU.min, ALU.mult))
            step(ts(cc(KO), tmp, s1, i2, ALU.mult, ALU.mult))
            step(ts(qscale[:], qscale[:], i1, None, ALU.mult))
            step(ts(qbias[:], qbias[:], i1, None, ALU.mult))
            step(ts(vrow[:], vrow[:], i1, None, ALU.mult))
            pr = ee[:].rearrange("p u n -> p (u n)")[:, 576:768]
            step(V.reciprocal(pr, prow[:, 0, :]))
            step(ts(prow[:, 0, :], prow[:, 0, :], s2, i3, ALU.mult, ALU.mult))
            step(ts(prow[:, 1, :], prow[:, 1, :], i3, None, ALU.mult))
            yw = y[:].rearrange("p u n -> p (u n)")[:, 0:1920].rearrange("p (t f) -> p t f", t=2)
            ys = flat16[0][:].bitcast(f32)[:, 0:960]
            step(V.reciprocal(ys, ys))
            for t_ in range(2):
                step(V.tensor_tensor(yw[:, t_, :], yw[:, t_, :], ys, ALU.mult))
            step(ts(yw, yw, MAGIC, MAGIC, ALU.add, ALU.subtract))
            step(ts(wqk[:], yw, 127.0, -128.0, ALU.min, ALU.max))
            ew = ee[:].rearrange("p u n -> p (u n)")[:, 0:576].rearrange("p (t f) -> p t f", t=3)
            for t_ in range(3):
                step(V.tensor_tensor(ew[:, t_, :], ew[:, t_, :], pr, ALU.mult))
            step(ts(ew, ew, MAGIC, MAGIC, ALU.add, ALU.subtract))
            step(ts(wp[:], ew, 127.0, -128.0, ALU.min, ALU.max))
            step(V.memset(bst[64:128, :], 0.0))
            assert n_prep[0] == PREP_DONE, n_prep[0]

            def norm(b, src, stt, agg, base_sig, i_stat, i_agg):
                for s in range(3):
                    last = V.bn_stats(stt[:, s, 0:6], src[:, s, :])
                last.then_inc(base_sig.sem, 1)
                ve.wait_ge(*base_sig.at(b, i_stat))
                plain(ve)
                for s in range(3):
                    last = V.bn_aggr(agg[:, s, :], stt[:, s, 0:6])
                last.then_inc(base_sig.sem, 1)
                ve.wait_ge(*base_sig.at(b, i_agg))

            def stage_a_pool(b, par, hp):
                ve.wait_ge(*a_tanh.at(b, 1))
                V.scalar_tensor_tensor(th[:], th[:], 1.0, dif[:], ALU.add, ALU.mult).then_inc(a_dve.sem, 1)
                ve.wait_ge(*a_dve.at(b, A_HD))
                ve.wait_ge(*a_keep.at(b - 2))
                V.scalar_tensor_tensor(h1[hp][:], th[:], 0.5, x[:, :, C:2 * C], ALU.mult, ALU.add
                                       ).then_inc(a_dve.sem, 1)
                ve.wait_ge(*a_dve.at(b, A_H))
                norm(b, h1[hp], stats, mv, a_dve, A_STAT, A_AGG)
                ts(vare[:, 0:3], mv[:, :, 1], EPS, None, ALU.add).then_inc(a_dve.sem, 1)

            def stage_a_split(b, hp):
                ve.wait_ge(*a_rstd.at(b))
                ve.wait_ge(*c_tT_ps.at(b - 3, 1))
                for s in range(3):
                    last = ts(xn[:, s, :], h1[hp][:, s, :], mv[:, s, 0:1], rstd[:, s:s + 1], ALU.subtract, ALU.mult)
                last.then_inc(a_dve.sem, 1)
                ve.wait_ge(*a_dve.at(b, A_XN))
                V.tensor_copy(hi, xn[:]).then_inc(a_split.sem, 1)
                ve.wait_ge(*a_split.at(b, 0))
                V.tensor_tensor(lo_rest, xn[:, :, 128:C], hi[:, :, 128:C], ALU.subtract)
                V.tensor_tensor(lo_main, xn[:, :, 0:128], hi[:, :, 0:128], ALU.subtract).then_inc(a_split.sem, 1)

            def round_qk(b, par, i):
                dst = (qT, kT)[i % 2][par][:, i // 2, :]
                ve.wait_ge(*a_qk.at(b, i - 1))
                ve.wait_ge(*a_qk_lin.at(b, i))
                ts(qr[:], qf[:], MAGIC, MAGIC, ALU.add, ALU.subtract).then_inc(a_qk_rnd.sem, 1)
                ve.wait_ge(*a_qk_rnd.at(b, i))
                if i < 2:
                    ve.wait_ge(*b_sc_ps.at(b - 2, 23))
                ts(dst, qr[:], 127.0, -128.0, ALU.min, ALU.max).then_inc(a_qk.sem, 1)

            def values(b, par, i):
                n = 2 - i
                ve.wait_ge(*a_v_ps.at(b, i))
                ve.wait_ge(*a_v_dve.at(b, 5 * i - 1))
                if i == 0:
                    ve.wait_ge(*v_av_ps.at(b - 2, 11))
                def row(j):
                    return vrow[:, j, :].unsqueeze(1).to_broadcast([128, n, C])
                ps = B_W[:, 0:192 * n].rearrange("p (s c) -> p s c", s=n)
                V.tensor_tensor(vf[:, 0:n, :], ps, row(0), ALU.mult).then_inc(a_v_dve.sem, 1)
                ve.wait_ge(*a_v_dve.at(b, 5 * i))
                V.tensor_tensor(vf[:, 0:n, :], vf[:, 0:n, :], row(1), ALU.add).then_inc(a_v_dve.sem, 1)
                ve.wait_ge(*a_v_dve.at(b, 5 * i + 1))
                ts(vf[:, 0:n, :], vf[:, 0:n, :], MAGIC, MAGIC, ALU.add, ALU.subtract).then_inc(a_v_dve.sem, 1)
                ve.wait_ge(*a_v_dve.at(b, 5 * i + 2))
                ts(vf[:, 0:n, :], vf[:, 0:n, :], 127.0, -128.0, ALU.min, ALU.max).then_inc(a_v_dve.sem, 1)
                ve.wait_ge(*a_v_dve.at(b, 5 * i + 3))
                heads = vf[:, 0:n, :].rearrange("p s (h e) -> p s h e", e=DH)
                if i == 0:
                    ts(vt[par][:, 0:2, :, 0:DH], heads, 2.0**64, None, ALU.mult).then_inc(a_v_dve.sem, 1)
                else:
                    for m in range(2):
                        last = ts(vt[par][:, 2 + m, :, 0:DH], heads[:, 0, :, :], vmask[:, m:m + 1], None, ALU.mult)
                    last.then_inc(a_v_dve.sem, 1)

            def softmax_part(b, g, s, par):
                yb, pp = y, pat
                sem = b_dve.sem
                if s == 0:
                    ve.wait_ge(*b_y.at(b, 8 * g + 7))
                    ts(ai[:], yb[:], MAGIC, -128.0, ALU.subtract, ALU.max).then_inc(sem, 1)
                    ve.wait_ge(*b_dve.at(b, NB * g + B_CLIP))
                    V.tensor_reduce(rmax[:], ai[:], AX.X, ALU.max).then_inc(sem, 1)
                    ve.wait_ge(*b_dve.at(b, NB * g + B_MAX))
                    ts(rmax[:], rmax[:], 127.0, None, ALU.min).then_inc(sem, 1)
                elif s == 1:
                    ve.wait_ge(*b_dve.at(b, NB * g + B_MCLIP))
                    V.tensor_tensor(ai[:], ai[:], rmax[:].unsqueeze(2).to_broadcast([128, UNITS, UW]), ALU.subtract
                                    ).then_inc(sem, 1)
                    ve.wait_ge(*b_dve.at(b, NB * g + B_SUB))
                    ts(ai[:], ai[:], 0.0, cc(CLAMP), ALU.min, ALU.max).then_inc(sem, 1)
                elif s == 2:
                    ve.wait_ge(*b_dve.at(b, NB * g + B_CLAMP))
                    ts(q1[:], ai[:], cc(NINVX), cc(Q1OFF), ALU.mult, ALU.add).then_inc(sem, 1)
                    ve.wait_ge(*b_dve.at(b, NB * g + B_Q1))
                    ts(xq[:], q1[:], HMAGIC, cc(KX), ALU.subtract, ALU.mult).then_inc(sem, 1)
                    ve.wait_ge(*b_dve.at(b, NB * g + B_XQ))
                    ts(q1[:].bitcast(i16), q1[:], -128.0, (HMAGIC + 127.0) * 128.0, ALU.mult, ALU.add).then_inc(sem, 1)
                    ve.wait_ge(*b_dve.at(b, NB * g + B_P2))
                    V.tensor_tensor(xq[:], ai[:], xq[:], ALU.add).then_inc(sem, 1)
                elif s == 3:
                    ve.wait_ge(*b_sq.at(b, g))
                    V.scalar_tensor_tensor(ee[:], ee[:], cc(CP), q1[:].bitcast(bf16), ALU.add, ALU.mult).then_inc(sem, 1)
                    ve.wait_ge(*b_dve.at(b, NB * g + B_E))
                    V.tensor_reduce(rsum[:], ee[:], AX.X, ALU.add).then_inc(sem, 1)
                    ve.wait_ge(*b_dve.at(b, NB * g + B_S))
                    ts(rsum[:], rsum[:], 0.25, None, ALU.mult).then_inc(sem, 1)
                    ve.wait_ge(*b_dve.at(b, NB * g + B_S4))
                    V.reciprocal(rs4[:], rsum[:]).then_inc(sem, 1)
                elif s == 6:
                    ve.wait_ge(*b_t4.at(b, g))
                    hi = ee[:].rearrange("p u n -> p (u n)").bitcast(u16).rearrange("p (n w) -> p n w", w=2)[:, :, 1]
                    ts(f4.rearrange("p u n -> p (u n)"), hi, 0x3F80, 0, ALU.bitwise_and, ALU.bitwise_or).then_inc(sem, 1)
                    ve.wait_ge(*b_dve.at(b, NB * g + B_F4))
                    V.scalar_tensor_tensor(ee[:], f4.bitcast(bf16), 6.0, ee[:], ALU.subtract, ALU.mult).then_inc(sem, 1)
                    ve.wait_ge(*b_dve.at(b, NB * g + B_T6))
                elif s == 7:
                    ve.wait_ge(*v_pt_ps.at(b, 4 * (g - 1) + 3))
                    hi = ee[:].rearrange("p u n -> p (u n)").bitcast(u16).rearrange("p (n w) -> p n w", w=2)[:, :, 1]
                    ts(pp[:, 0:GW].bitcast(u16), hi, 0x7F80, 0, ALU.bitwise_and, ALU.bitwise_or).then_inc(sem, 1)
                    ve.wait_ge(*b_dve.at(b, NB * g + B_MASK))
                    ts(pp[:, 0:GW], pp[:, 0:GW], 115.0 * 128.0, 0.0, ALU.subtract, ALU.max).then_inc(sem, NB - 16)

            def attention_out(b, g):
                ve.wait_ge(*v_o.at(b, g - 1))
                ve.wait_ge(*v_lin.at(b, g))
                ts(orr[:], of[:], MAGIC, -128.0, ALU.subtract, ALU.max).then_inc(v_rnd.sem, 1)
                ve.wait_ge(*v_rnd.at(b, g))
                if g == 0:
                    ve.wait_ge(*c_proj_ps.at(b - 1, 1))
                ts(oT[:, g, :], orr[:], 127.0, None, ALU.min).then_inc(v_o.sem, 1)

            def c_project(b, i):
                ve.wait_ge(*c_proj_ps.at(b, i))
                n = 2 - i
                V.tensor_tensor(pf[:, 2 * i:2 * i + n, :], B_W[:, 0:192 * n].rearrange("p (s c) -> p s c", s=n),
                                prow[:, 0, :].unsqueeze(1).to_broadcast([128, n, C]), ALU.mult).then_inc(c_dve.sem, 1)

            def c_residual(b):
                sem = c_dve.sem
                ve.wait_ge(*a_keep.at(b))
                ve.wait_ge(*c_dve.at(b, C_PROJ1))
                V.tensor_tensor(pf[:], pf[:], prow[:, 1, :].unsqueeze(1).to_broadcast([128, 3, C]), ALU.add).then_inc(sem, 1)
                ve.wait_ge(*c_dve.at(b, C_BIAS))
                ts(pf[:], pf[:], MAGIC, MAGIC, ALU.add, ALU.subtract).then_inc(sem, 1)
                ve.wait_ge(*c_dve.at(b, C_RND))
                ts(pf[:], pf[:], 127.0, -128.0, ALU.min, ALU.max).then_inc(sem, 1)
                ve.wait_ge(*c_dve.at(b, C_CLIP))
                V.scalar_tensor_tensor(h2[:], pf[:], s3, hres[:], ALU.mult, ALU.add).then_inc(sem, 1)
                ve.wait_ge(*c_dve.at(b, C_H2))
                norm(b, h2, cstats, cmv, c_dve, C_STAT, C_AGG)
                ts(cvar[:, 0:3], cmv[:, :, 1], EPS, None, ALU.add).then_inc(sem, 1)

            def c_rms(b):
                sem = c_dve.sem
                ve.wait_ge(*c_rstd.at(b, 0))
                V.tensor_tensor(cvar2[:, 0:3], cmv[:, :, 1], crstd[:, 0:3], ALU.mult).then_inc(sem, 1)
                ve.wait_ge(*c_dve.at(b, C_V1))
                V.tensor_tensor(cvar2[:, 0:3], cvar2[:, 0:3], crstd[:, 0:3], ALU.mult).then_inc(sem, 1)

            def c_split(b, rp):
                sem = c_dve.sem
                for s in range(3):
                    last = ts(cn[:, s, :], h2[:, s, :], cmv[:, s, 0:1], crstd[:, s:s + 1], ALU.subtract, ALU.mult)
                last.then_inc(sem, 1)
                ve.wait_ge(*c_dve.at(b, C_XN))
                ve.wait_ge(*c_rstd.at(b, 1))
                for s in range(3):
                    last = ts(ct[:, s, :], cn[:, s, :], crstd2[:, s:s + 1], None, ALU.mult)
                last.then_inc(sem, 1)
                ve.wait_ge(*c_dve.at(b, C_T))
                ve.wait_ge(*a_xT_ps.at(b + 2, 1)) if not isinstance(b, int) or b + 2 < BLOCKS else None
                V.tensor_copy(hi, ct[:]).then_inc(sem, 1)
                ve.wait_ge(*c_dve.at(b, C_HI))
                V.tensor_tensor(lo_rest, ct[:, :, 128:C], hi[:, :, 128:C], ALU.subtract)
                V.tensor_tensor(lo_main, ct[:, :, 0:128], hi[:, :, 0:128], ALU.subtract).then_inc(sem, 1)
                V.tensor_tensor(res[rp][:], h2[:], cn[:], ALU.add).then_inc(sem, 1)

            def c_top(b):
                sem = c_dve.sem
                ve.wait_ge(*c_gate_ps.at(b))
                ts(g20[:, :, 0:EXPERTS], B_W[:, 0:48].rearrange("p (s e) -> p s e", s=3), 1.0 / WSCALE, None, ALU.mult
                   ).then_inc(sem, 1)
                ve.wait_ge(*c_dve.at(b, C_GATE))
                plain(ve)
                for s in range(3):
                    last = V.max(top8[:, s, :], g20[:, s, 0:EXPERTS])
                last.then_inc(sem, 1)
                ve.wait_ge(*c_dve.at(b, C_TOP))
                V.tensor_copy(rep8[:, :, 0:TOPK], top8[:, :, 0:TOPK]).then_inc(sem, 1)
                ve.wait_ge(*c_dve.at(b, C_REP))
                plain(ve)
                for s in range(3):
                    last = V.match_replace(gz[:, s, :], rep8[:, s, :], g20[:, s, :], -BIG)
                last.then_inc(sem, 1)
                ve.wait_ge(*c_dve.at(b, C_MR))
                V.tensor_tensor(gm[:], gz[:, :, 0:EXPERTS], g20[:, :, 0:EXPERTS], ALU.is_lt).then_inc(sem, 1)
                V.tensor_tensor(gd[:], g20[:, :, 0:EXPERTS], top8[:, :, 0:1].to_broadcast([128, 3, EXPERTS]), ALU.subtract
                                ).then_inc(sem, 1)

            def c_weights(b):
                sem = c_dve.sem
                ve.wait_ge(*c_tanh.at(b))
                ts(gn[:], gt[:], 1.0, None, ALU.add).then_inc(sem, 1)
                ts(gr[:], gt[:], -1.0, 1.0, ALU.mult, ALU.add).then_inc(sem, 1)
                ve.wait_ge(*c_dve.at(b, C_DEN))
                V.reciprocal(gr[:], gr[:]).then_inc(sem, 1)
                ve.wait_ge(*c_dve.at(b, C_RCP))
                V.tensor_tensor(gn[:], gn[:], gr[:], ALU.mult).then_inc(sem, 1)
                ve.wait_ge(*c_dve.at(b, C_E1))
                V.tensor_tensor(gn[:], gn[:], gm[:], ALU.mult).then_inc(sem, 1)
                ve.wait_ge(*c_dve.at(b, C_E2))
                V.tensor_reduce(gs[:, 0:3], gn[:], AX.X, ALU.add).then_inc(sem, 1)
                ve.wait_ge(*c_dve.at(b, C_SUM))
                V.reciprocal(gsr[:, 0:3], gs[:, 0:3]).then_inc(sem, 1)
                ve.wait_ge(*c_dve.at(b, C_SR))
                V.tensor_tensor(gw[:, :, 32:48], gn[:], gsr[:, 0:3].unsqueeze(2).to_broadcast([128, 3, EXPERTS]), ALU.mult
                                ).then_inc(sem, 1)
                ve.wait_ge(*c_dve.at(b, C_W))
                V.tensor_copy(gh16[:], gw[:, :, 32:48]).then_inc(sem, 1)
                ve.wait_ge(*c_dve.at(b, C_H16))
                V.tensor_copy(gw[:, :, 0:16], gh16[:]).then_inc(sem, 1)
                V.tensor_tensor(gw[:, :, 16:32], gw[:, :, 32:48], gh16[:], ALU.subtract).then_inc(sem, 1 + NC_ - 33)

            def tile(b, t):
                ve.wait_ge(*d_l_ps.at(b, t))
                ve.wait_ge(*d_act.at(b, t - 2))
                ts(lc[t % 2][:], B_L[:, 0:COLS], (LIMIT + 1.0) * WSCALE, (1.0 - LIMIT) * WSCALE, ALU.min, ALU.max
                   ).then_inc(d_lc.sem, 1)
                ve.wait_ge(*d_w_ps.at(b, t))
                ve.wait_ge(*d_u.at(b, t))
                V.scalar_tensor_tensor(p[t % 2][:], u[t % 2][:], GLU_MAX, B_W[:, 0:COLS], ALU.min, ALU.mult
                                       ).then_inc(d_p.sem, 1)

            def finish(b, rp):
                ve.wait_ge(*d_y_ps.at(b, TILES - 1))
                v = (b) * 64
                if not isinstance(b, int) or b > 0:
                    ve.wait_ge(stored.sem, v)
                V.tensor_tensor(yo[:, 0:2, :], B_Y0[:, 0:384].rearrange("p (s c) -> p s c", s=2), res[rp][:, 0:2, :],
                                ALU.add).then_inc(d_out.sem, 1)
                V.tensor_tensor(yo[:, 2, :], B_Y1[:, 0:192], res[rp][:, 2, :], ALU.add).then_inc(d_out.sem, 1)

            def split_weights():
                for c in range(9):
                    n = 768 if c < 8 else EXPERTS
                    cs = slice(768 * c, 768 * c + n)
                    ve.wait_ge(w_loaded.sem, 48 * (c + 1))
                    for i in range(2):
                        ts(wtmp[i][:, 0:n], wst[:, i, 0:n], lnscale[:, i:i + 1], WSCALE, ALU.mult, ALU.mult)
                    if c < 8:
                        ts(bs[64:128, 0:384], bst[64:128, 0:384], WSCALE, None, ALU.mult)
                        last = ts(bs[64:128, 384:768], bst[64:128, 384:768], 1.0, WSCALE, ALU.add, ALU.mult)
                    else:
                        last = ts(bs[64:128, 0:n], bst[64:128, 0:n], WSCALE, None, ALU.mult)
                    last.then_inc(w_high.sem, 1)
                    ve.wait_ge(w_high.sem, c + 1)
                    V.tensor_copy(w1l5[64:96, cs], bs[64:96, 0:n])
                    V.tensor_copy(bh[96:128, 0:n], bs[96:128, 0:n]).then_inc(w_split.sem, 1)
                    ve.wait_ge(w_split.sem, c + 1)
                    ve.wait_ge(prep_act.sem, c + 2)
                    V.tensor_tensor(w1l5[96:128, cs], bs[96:128, 0:n], bh[96:128, 0:n], ALU.subtract)
                    V.tensor_tensor(w1l0[:, cs], wtmp[0][:, 0:n], w1h0[:, cs], ALU.subtract)
                    V.tensor_tensor(w1l5[0:64, cs], wtmp[1][0:64, 0:n], w1hR[0:64, cs], ALU.subtract
                                    ).then_inc(w_ready.sem, 1)

            def body(k, par):
                if isinstance(k, int) and k == 0:
                    split_weights()
                d, dp = k - 2, par
                for t in range(STEPS):
                    if t == 0 and runs(d - 1):
                        tile(d - 1, TILES - 1)
                    if t >= 1 and runs(d):
                        tile(d, t - 1)
                    if t == 3 and runs(d - 1):
                        finish(d - 1, (dp + 1) % 2)
                    for b, g, s in b_steps(k, t):
                        softmax_part(b, g, s, par if t >= 8 else (par + 1) % 2)
                    if t == 5 and runs(k + 1):
                        stage_a_pool(k + 1, (par + 1) % 2, (par + 1) % 2)
                    if t == 8 and runs(k + 1):
                        stage_a_split(k + 1, (par + 1) % 2)
                    if t in (11, 12, 13, 16) and runs(k + 1):
                        round_qk(k + 1, (par + 1) % 2, (11, 12, 13, 16).index(t))
                    if t in (6, 7) and runs(k):
                        round_qk(k, par, t - 2)
                    if t in (2, 5) and runs(k):
                        values(k, par, t // 5)
                    if t == 21 and runs(k):
                        attention_out(k, 0)
                    if t in (5, 13) and runs(k - 1):
                        attention_out(k - 1, 1 + t // 13)
                    if runs(k - 1):
                        if t in (14, 15):
                            c_project(k - 1, t - 14)
                        if t == 15:
                            c_residual(k - 1)
                        if t == 16:
                            c_rms(k - 1)
                        if t == 17:
                            c_split(k - 1, (par + 1) % 2)
                        if t == 20:
                            c_top(k - 1)
                        if t == 21:
                            c_weights(k - 1)

            bodies(ve, body)


def constants():
    sel = np.zeros((32, TILES, 128), np.float16)
    for pair in range(EXPERTS // 2):
        for j in range(3):
            for half in range(2):
                e = 2 * pair + (j if j < 2 else half)
                for part in (0, EXPERTS):
                    sel[part + e, 3 * pair + j, 64 * half:64 * half + 64] = 1.0 / WSCALE
    vmask = np.zeros((128, 2), np.float32)
    for b, (first, end) in enumerate(REST_ROWS):
        vmask[first:end, b] = 2.0**64
    return {"vmask": vmask, "id16": np.eye(128, dtype=np.float16), "id32": np.eye(128, dtype=np.float32),
            "sel": sel.reshape(32, TILES * 128)}


def expert_columns(w):
    halves = w.reshape(*w.shape[:-2], EXPERTS // 2, 2, 2, C)
    main = np.moveaxis(halves[..., 0:128], -3, -2)
    rest = np.moveaxis(halves[..., 128:C], -3, -2)
    main = main.reshape(*main.shape[:-2], 256)
    rest = rest.reshape(*rest.shape[:-2], 128)
    out = np.concatenate([main, rest], axis=-1)
    return out.reshape(*w.shape[:-2], EXPERTS * 384)


def rows_128_64(w):
    return np.stack([w[0:128], np.concatenate([w[128:192], w[128:192]])], axis=1)


def pad_heads(w):
    z = np.zeros((HEADS, 32) + w.shape[1:], w.dtype)
    z[:, 0:DH] = w.reshape((HEADS, DH) + w.shape[1:])
    return z.reshape((HEADS * 32,) + w.shape[1:])


def kernel(**inputs):
    import concourse.bacc as bacc
    from concourse.bass_utils import run_bass_kernel_spmd

    i = {n: np.asarray(v) for n, v in inputs.items()}
    g = lambda n: i[n]
    wqkv, sw, bq = g("L0_attn_w_qkv"), g("L0_attn_sw_qkv"), g("L0_attn_b_qkv")
    wq, wk, wv = (wqkv[C * n:C * n + C] for n in range(3))

    def pad_scale(s):
        z = np.ones((HEADS, 32), s.dtype)
        z[:, 0:DH] = s.reshape(HEADS, DH)
        return z.reshape(-1)

    w1 = np.moveaxis(g("L0_ffn_w1"), 0, 1)
    w1 = np.concatenate([expert_columns(w1), g("L0_ffn_gate_w").T], axis=1)
    b1 = np.concatenate([expert_columns(g("L0_ffn_b1")), g("L0_ffn_gate_b")])[None, :]
    w2 = g("L0_ffn_w2").reshape(EXPERTS // 2, 2, C, C)
    w2 = np.concatenate([w2[:, 0, 0:128], w2[:, 1, 0:128], w2[:, 0, 128:C], w2[:, 1, 128:C]], axis=1)
    w2 = w2.reshape(TILES, 128, C).transpose(1, 0, 2)
    wp = pad_heads(g("L0_attn_w_proj").T).reshape(3, 128, C).transpose(1, 0, 2)
    arrays = {
        "x": g("x").reshape(BATCH, SEQ * C),
        "tokw": g("L0_tok_w"),
        "scal": np.concatenate([g("L0_attn_s_a1"), g("L0_attn_s_attn"), g("L0_attn_s_a2"), g("L0_attn_s_a3")])[None, :],
        "wqk": rows_128_64(np.concatenate([pad_heads(wq), pad_heads(wk), wv]).T),
        "sw_row": np.concatenate([pad_scale(sw[0:C]), pad_scale(sw[C:2 * C]), sw[2 * C:]])[None, :],
        "bv_row": bq[2 * C:][None, :],
        "wp": wp,
        "sp_row": g("L0_attn_sw_proj")[None, :],
        "bp_row": g("L0_attn_b_proj")[None, :],
        "lnscale": np.stack([g("L0_ffn_scale")[0:128], np.concatenate([g("L0_ffn_scale")[128:192]] * 2)], axis=1),
        "b2": g("L0_ffn_b2"),
        "w2": w2,
        "w1": rows_128_64(w1),
        "b1": b1,
        **constants(),
    }

    def cols(v):
        return np.concatenate([pad_heads(v[0:C]), pad_heads(v[C:2 * C])]).reshape(6, 128).T
    arrays["sw_col"], arrays["b_col"] = cols(sw), cols(bq)
    arrays = {n: np.ascontiguousarray(v) for n, v in arrays.items()}

    nc = bacc.Bacc("TRN2", target_bir_lowering=False, num_devices=1)
    aps = {n: nc.dram_tensor(f"in_{n}", v.shape, mybir.dt.from_np(v.dtype), kind="ExternalInput").ap()
           for n, v in arrays.items()}
    aps["out"] = nc.dram_tensor("out_0", (BATCH, TOK, C), mybir.dt.float32, kind="ExternalOutput").ap()
    build(nc, aps)
    r = run_bass_kernel_spmd(nc, [{f"in_{n}": v for n, v in arrays.items()}], core_ids=[0])
    return r.results[0]["out_0"]
```

```python
from contextlib import ExitStack

import concourse.bass as bass
import numpy as np
from concourse import mybir

BATCH, SEQ, C = 64, 375, 192
TOK = (SEQ - 2) // 2 + 1
REST = TOK - 128
BLOCKS = BATCH // 2
HEADS, DH = 12, 16
EXPERTS, TOPK = 16, 4
PAD = 64 - REST
REST_ROWS = ((0, REST), (64 + PAD, 128))
COLS = 384
SLOT_COL = (0, 256, 128)
KEY_COL = (0, 192 + PAD)
TILES = EXPERTS * 3 // 2
STEPS = 24
RING, LRING = 6, 3
GROUPS, GH = 3, 4
UNITS = 3 * GH
UW = TOK
HALF = (UW + 1) // 2
SHARE = UNITS // 2
GW = UNITS * UW
W1COLS = TILES * 256 + EXPERTS
WSCALE = 64.0
MAGIC = 1.5 * 2.0**23
HMAGIC = 1536.0
BIG = 3.0e38
LIMIT, ALPHA = 7.0, 1.702
GLU_MAX = LIMIT / (1.0 + float(np.exp(-ALPHA * LIMIT)))
EPS = 1e-5

LOOP_FROM, LOOP_TO = 4, 30
LAST_BODY = BLOCKS + 2


def build(nc, a):
    dt, ALU, ACT, AX = mybir.dt, mybir.AluOpType, mybir.ActivationFunctionType, mybir.AxisListType
    f32, f16, bf16, u16, i16 = dt.float32, dt.float16, dt.bfloat16, dt.uint16, dt.int16
    ctx = ExitStack()
    with ctx:
        def sb(name, shape, d):
            return ctx.enter_context(nc.sbuf_tensor(name, shape, d))

        class Signal:

            def __init__(self, name, per=1):
                self.sem, self.per = ctx.enter_context(nc.semaphore(name)), per

            def at(self, b, i=0):
                v = b * self.per + (i + 1)
                return (prep.sem, 1) if isinstance(v, int) and v <= 0 else (self.sem, v)

        def plain(eng):
            eng.sem_inc(taken.sem, 1)

        id16 = sb("id16", [128, 128], f16)
        id32 = sb("id32", [128, 128], f32)
        sel = sb("sel", [32, TILES * 128], f16)
        tokw = sb("tokw", [128, 2, C], f32)
        wqk = sb("wqk", [128, 2, 960], f16)
        wp = sb("wp", [128, 3, C], f16)
        w1h0 = sb("w1h0", [128, W1COLS], f16)
        w1hR = sb("w1hR", [128, W1COLS], f16)
        w1l0 = sb("w1l0", [128, W1COLS], f16)
        w1l5 = sb("w1l5", [128, W1COLS], f16)
        w2 = sb("w2", [128, TILES, C], f32)
        b2 = sb("b2", [48, C], f32)
        scal = sb("scal", [128, 4], f32)
        iscal = sb("iscal", [128, 4], f32)
        consts = sb("consts", [128, 32], f32)
        qscale = sb("qscale", [128, 6], f32)
        qbias = sb("qbias", [128, 6], f32)
        vrow = sb("vrow", [128, 2, C], f32)
        prow = sb("prow", [128, 2, C], f32)
        lnscale = sb("lnscale", [128, 2], f32)
        vmask = sb("vmask", [128, 2], f32)
        negh = sb("negh", [128, 4], f32)
        magic = sb("magic", [128, 1], f32)
        lift = sb("lift", [128, 1], f32)
        hmagic = sb("hmagic", [128, 1], f32)
        x = sb("x", [128, 3, 2 * C], f32)
        dif = sb("dif", [128, 3, C], f32)
        dT = sb("dT", [128, 2, COLS], f32)
        th = sb("th", [128, 3, C], f32)
        h1 = [sb(f"h1{i}", [128, 3, C], f32) for i in range(2)]
        hres = sb("hres", [128, 3, C], f32)
        xn = th
        split = sb("split", [128, 3, 2 * C], f16)
        hi, lo_rest, lo_main = split[:, :, 0:C], split[:, :, C:256], split[:, :, 256:384]
        xT = sb("xT", [128, 3, COLS], f16)
        stats = sb("stats", [128, 3, 8], f32)
        mv = sb("mv", [128, 3, 2], f32)
        vare = sb("vare", [128, 4], f32)
        rstd = sb("rstd", [128, 4], f32)
        qf = sb("qf", [128, COLS], f32)
        qr = sb("qr", [128, COLS], f16)
        qT = [sb(f"qT{i}", [128, 3, COLS], f16) for i in range(2)]
        kT = [sb(f"kT{i}", [128, 3, COLS], f16) for i in range(2)]
        vt = [sb(f"vt{i}", [128, 4, HEADS, 32], bf16) for i in range(2)]
        flat16 = [sb(n, [128, GW], f16) for n in ("ai0", "ai1", "q1", "xq")]
        ai0, ai1, q1, xq = (v[:].rearrange("p (u n) -> p u n", u=UNITS) for v in flat16)
        ee = sb("ee", [128, UNITS, UW], f32)
        ai = (ai0, ai1)
        f4 = q1[:].bitcast(u16)
        pat = sb("pat", [128, GW + 12], i16)
        rmax = sb("rmax", [128, UNITS], f32)
        nmax = sb("nmax", [128, UNITS], f32)
        rsum = sb("rsum", [128, UNITS], f32)
        rs4 = sb("rs4", [128, UNITS], f32)
        pt = [sb(f"pt{i}", [128, 288], f32) for i in range(2)]
        of = sb("of", [128, COLS], f32)
        orr = sb("orr", [128, COLS], f16)
        oT = sb("oT", [128, GROUPS, COLS], f16)
        pf = sb("pf", [128, 3, C], f32)
        vf = pf
        h2 = sb("h2", [128, 3, C], f32)
        cn = th
        ct = pf
        cstats = sb("cstats", [128, 3, 8], f32)
        cmv = sb("cmv", [128, 3, 2], f32)
        cvar = sb("cvar", [128, 4], f32)
        crstd = sb("crstd", [128, 4], f32)
        cvar2 = sb("cvar2", [128, 4], f32)
        crstd2 = sb("crstd2", [128, 4], f32)
        res = [sb(f"res{i}", [128, 3, C], f32) for i in range(2)]
        tT = [sb(f"tT{i}", [128, 4, COLS], f16) for i in range(2)]
        g20 = sb("g20", [128, 3, 20], f32)
        gz = sb("gz", [128, 3, 20], f32)
        top8 = sb("top8", [128, 3, 8], f32)
        rep8 = sb("rep8", [128, 3, 8], f32)
        gm = sb("gm", [128, 3, EXPERTS], f32)
        gd = sb("gd", [128, 3, EXPERTS], f32)
        gt = sb("gt", [128, 3, EXPERTS], f32)
        gn = sb("gn", [128, 3, EXPERTS], f32)
        gr = sb("gr", [128, 3, EXPERTS], f32)
        gs = sb("gs", [128, 4], f32)
        gsr = sb("gsr", [128, 4], f32)
        gw = sb("gw", [128, 3, 48], f32)
        gh16 = sb("gh16", [128, 3, EXPERTS], f16)
        wT32 = [sb(f"wT32{i}", [48, COLS], f32) for i in range(2)]
        wT16 = [w[0:32, 0:COLS // 2].bitcast(f16) for w in wT32]
        u = [sb(f"u{i}", [128, COLS], f32) for i in range(RING)]
        lin = [sb(f"lin{i}", [128, COLS], f32) for i in range(LRING)]
        wb = [sb(f"wb{i}", [128, COLS], f32) for i in range(LRING)]
        yo = sb("yo", [128, 3, C], f32)
        wst = ee[:].rearrange("p u n -> p (u n)")[:, 0:1536].rearrange("p (t f) -> p t f", t=2)
        wtmp = [v[:].bitcast(f32) for v in flat16[2:]]
        bst = flat16[0][:].bitcast(f32)[:, 0:768]
        bs = flat16[1][:].bitcast(f32)[:, 0:768]
        bh = pat[:, 0:768].bitcast(f16)

        bank = [ctx.enter_context(nc.psum_tensor(f"bank{i}", [128, 512], f32)) for i in range(8)]
        B_SC, B_PT, B_AV, B_Y1, B_G, B_L, B_W, B_Y0 = bank

        ld_const = Signal("ld_const")
        x_loaded = Signal("x_loaded")
        w_loaded = Signal("w_loaded")
        stored = Signal("stored")
        prep = Signal("prep")
        prep_act = Signal("prep_act")
        w_ready = Signal("w_ready")
        w_high = Signal("w_high")
        w_split = Signal("w_split")
        a_keep = Signal("a_keep")
        taken = Signal("taken")
        a_dif = Signal("a_dif")
        a_difT_ps = Signal("a_difT_ps", 2)
        a_difT = Signal("a_difT", 2)
        a_sc_ps = Signal("a_sc_ps", 2)
        a_tanh = Signal("a_tanh", 2)
        a_dve = Signal("a_dve", 6)
        a_rstd = Signal("a_rstd")
        a_split = Signal("a_split", 2)
        a_xT_ps = Signal("a_xT_ps", 2)
        a_xT = Signal("a_xT", 2)
        a_qk_ps = Signal("a_qk_ps", 6)
        a_qk_lin = Signal("a_qk_lin", 6)
        a_qk_rnd = Signal("a_qk_rnd", 6)
        a_qk = Signal("a_qk", 6)
        a_v_ps = Signal("a_v_ps", 2)
        a_v_act = Signal("a_v_act", 2)
        a_v_lin = Signal("a_v_lin", 2)
        a_v_dve = Signal("a_v_dve", 3)
        b_sc_ps = Signal("b_sc_ps", 24)
        b_y = Signal("b_y", 24)
        b_dve = Signal("b_dve", 3 * 18)
        b_sq = Signal("b_sq", 3)
        b_t4 = Signal("b_t4", 3)
        b_t4_act = Signal("b_t4_act", 3)
        b_sub = Signal("b_sub", 3)
        v_pt_ps = Signal("v_pt_ps", 12)
        v_pt = Signal("v_pt", 12)
        v_av_ps = Signal("v_av_ps", 12)
        v_lin = Signal("v_lin", 3)
        v_rnd = Signal("v_rnd", 3)
        v_o = Signal("v_o", 3)
        c_proj_ps = Signal("c_proj_ps", 2)
        c_proj = Signal("c_proj", 2)
        c_gate = Signal("c_gate")
        c_res = Signal("c_res")
        c_dve = Signal("c_dve", 40)
        c_rstd = Signal("c_rstd", 4)
        c_tT_ps = Signal("c_tT_ps", 2)
        c_tT = Signal("c_tT", 3)
        c_gate_ps = Signal("c_gate_ps")
        c_tanh = Signal("c_tanh")
        c_wT_ps = Signal("c_wT_ps")
        c_wT = Signal("c_wT", 2)
        d_g_ps = Signal("d_g_ps", TILES)
        d_l_ps = Signal("d_l_ps", TILES)
        d_w_ps = Signal("d_w_ps", TILES)
        d_u = Signal("d_u", TILES)
        d_v = Signal("d_v", TILES)
        d_w = Signal("d_w", TILES)
        d_p = Signal("d_p", TILES)
        d_half = Signal("d_half", TILES)
        d_act = Signal("d_act", TILES)
        d_y_ps = Signal("d_y_ps", TILES)
        d_sum = Signal("d_sum", 2)
        d_out = Signal("d_out")

        KAPPA, KX, NINVX, Q1OFF, CLAMP, HB, CP, KO, KP3, S3C = range(10)

        def cc(i):
            return consts[:, i:i + 1]

        def runs_a(k):
            return not isinstance(k, int) or 0 <= k + 1 < BLOCKS

        def runs(b):
            return not isinstance(b, int) or 0 <= b < BLOCKS

        def slot_cols(t2d, s):
            return t2d[:, SLOT_COL[s]:SLOT_COL[s] + 128]

        A_HD, A_H, A_STAT, A_AGG, A_VAR, A_XN = range(6)
        (B_CLIP, B_HALF, B_MAX, B_NEG, B_SUB, B_CLAMP, B_Q1, B_XQ, B_P2, B_R, B_E, B_S, B_S4, B_RS4, B_F4, B_T6,
         B_MASK, B_PAT) = range(18)
        NB = 18
        (C_SCALE, C_BIAS, C_RND, C_CLIP, C_H2, C_STAT, C_AGG, C_VAR, C_XN, C_T, C_HI, C_LO,
         C_TOP, C_REP, C_MR, C_MASK, C_D, C_NUM, C_DEN, C_RCP, C_E1, C_E2, C_SUM, C_SR, C_W,
         C_H16, C_HI32, C_LO32) = range(28)
        NC_ = 40

        def b_steps(k, t):
            g, s = t // 8 - 1, t % 8
            b = k
            if g < 0:
                b, g = k - 1, GROUPS - 1
            return [(b, g, s)] if runs(b) else []

        def v_steps(k, t):
            if t < 0:
                return []
            b, g, i = {0: (k - 1, 1, t), 1: (k - 1, 2, t - 8), 2: (k, 0, t - 16)}[t // 8]
            return [(b, g, i)] if i < GH and runs(b) else []

        PREP_DONE = 44
        block = ctx.enter_context(nc.Block())

        def bodies(eng, body):
            for k in range(-1, LOOP_FROM):
                body(k, k % 2)
            with eng.Fori(0, (LOOP_TO - LOOP_FROM) // 2) as turn:
                body(turn * 2 + LOOP_FROM, 0)
                body(turn * 2 + (LOOP_FROM + 1), 1)
            for k in range(LOOP_TO, LAST_BODY + 1):
                body(k, k % 2)

        N_CONST = 19

        @block.sync
        def _(sp):
            for dst, src in [
                (id16[:], a["id16"]), (id32[:], a["id32"]), (sel[:], a["sel"]),
                (tokw[:, 0, :], a["tokw"][0:128, :]), (tokw[0:64, 1, :], a["tokw"][128:192, :]),
                (scal[:], a["scal"].to_broadcast([128, 4])),
                (qscale[:], a["sw_col"]), (qbias[:], a["b_col"]),
                (ee[:].rearrange("p u n -> p (u n)")[:, 0:1920].rearrange("p (t f) -> p t f", t=2), a["wqk"]),
                (flat16[0][:].bitcast(f32)[:, 0:960], a["sw_row"].to_broadcast([128, 960])),
                (vrow[:, 0, :], a["sw_row"][:, 768:960].to_broadcast([128, C])),
                (vrow[:, 1, :], a["bv_row"].to_broadcast([128, C])),
                (flat16[1][:].bitcast(f32)[:, 0:576].rearrange("p (t f) -> p t f", t=3), a["wp"]),
                (prow[:, 0, :], a["sp_row"].to_broadcast([128, C])),
                (prow[:, 1, :], a["bp_row"].to_broadcast([128, C])),
                (lnscale[:], a["lnscale"]), (vmask[:], a["vmask"]), (b2[32:48, :], a["b2"]), (w2[:, :, :], a["w2"]),
                            ]:
                sp.dma_start(dst, src).then_inc(ld_const.sem, 16)

            def load_x(b):
                sp.wait_ge(*a_dve.at(b - 1, A_H))
                for i in range(2):
                    row = a["x"][b * 2 + i, :]
                    sp.dma_start(x[:, i, :], row[0:128 * 2 * C].rearrange("(n f) -> n f", f=2 * C)
                                 ).then_inc(x_loaded.sem, 16)
                    sp.dma_start(x[REST_ROWS[i][0]:REST_ROWS[i][1], 2, :],
                                 row[128 * 2 * C:TOK * 2 * C].rearrange("(n f) -> n f", f=2 * C)
                                 ).then_inc(x_loaded.sem, 16)

            def store(b):
                sp.wait_ge(*d_out.at(b))
                for i in range(2):
                    sp.dma_start(a["out"][b * 2 + i, 0:128, :], yo[:, i, :]).then_inc(stored.sem, 16)
                    sp.dma_start(a["out"][b * 2 + i, 128:TOK, :], yo[REST_ROWS[i][0]:REST_ROWS[i][1], 2, :]
                                 ).then_inc(stored.sem, 16)

            sp.wait_ge(prep.sem, 1)
            load_x(0)

            def body(k, par):
                if isinstance(k, int) and k == 0:
                    sp.wait_ge(prep.sem, PREP_DONE)
                    for c in range(9):
                        if c:
                            sp.wait_ge(w_high.sem, c)
                        n = 768 if c < 8 else EXPERTS
                        sp.dma_start(wst[:, :, 0:n], a["w1"][:, :, 768 * c:768 * c + n]).then_inc(w_loaded.sem, 16)
                        for r in (64, 96):
                            sp.dma_start(bst[r:r + 1, 0:n], a["b1"][:, 768 * c:768 * c + n]).then_inc(w_loaded.sem, 16)
                if runs(k + 2):
                    load_x(k + 2)
                if runs(k - 3):
                    store(k - 3)

            bodies(sp, body)
            sp.wait_ge(stored.sem, 64 * BLOCKS)

        def misc_jobs(k, t):
            jobs = []
            if runs(k + 1):
                A = {0: ("difT0", a_difT, 0), 1: ("difT1", a_difT, 1), 3: ("sc0", a_tanh, 0), 4: ("sc1", a_tanh, 1),
                     10: ("xT0", a_xT, 0), 11: ("xT1", a_xT, 1), 12: ("qk0", a_qk_lin, 0), 15: ("qk1", a_qk_lin, 1),
                     17: ("qk2", a_qk_lin, 2), 22: ("qk3", a_qk_lin, 3)}
                if t in A:
                    jobs.append((A[t][0], k + 1, A[t][1], A[t][2]))
            if runs(k):
                A2 = {2: ("v0", a_v_act, 0), 5: ("v1", a_v_act, 1), 6: ("qk4", a_qk_lin, 4), 8: ("qk5", a_qk_lin, 5)}
                if t in A2:
                    jobs.append((A2[t][0], k, A2[t][1], A2[t][2]))
            if runs(k - 1):
                if t == 14:
                    jobs.append(("pr0", k - 1, c_proj, 0))
                Cs = {14: ("pr1", c_proj, 1), 18: ("tT0", c_tT, 0),
                      19: ("tT1", c_tT, 2), 20: ("gate", c_gate, 0), 23: ("wT", c_wT, 1)}
                if t in Cs:
                    jobs.append((Cs[t][0], k - 1, Cs[t][1], Cs[t][2]))
            return jobs

        @block.tensor
        def _(pe):
            mm = nc.tensor.matmul
            last_reader = [None]

            def claim_w(k):
                if last_reader[0] is not None:
                    sig, off, i = last_reader[0]
                    pe.wait_ge(*sig.at(k + off, i))

            def misc(k, par, name, b, bpar):
                if name in ("difT0", "difT1"):
                    if name == "difT0":
                        pe.wait_ge(*a_dif.at(b))
                    for s in range(3):
                        c0, n = (0, 128) if name == "difT0" else (128, 64)
                        out = slot_cols(B_W[0:n, 0:COLS], s)
                        last = nc.tensor.transpose(out, dif[:, s, c0:c0 + n], id32[:])
                    last.then_inc(a_difT_ps.sem, 1)
                elif name in ("sc0", "sc1"):
                    pe.wait_ge(*a_difT.at(b, 1))
                    for s in ((0, 1) if name == "sc0" else (2,)):
                        o = B_W[:, 192 * (s % 2):192 * (s % 2) + 192]
                        mm(o, slot_cols(dT[:, 0, :], s), tokw[:, 0, :], start=True, stop=False)
                        last = mm(o, slot_cols(dT[0:64, 1, :], s), tokw[0:64, 1, :], start=False, stop=True)
                    last.then_inc(a_sc_ps.sem, 1)
                elif name in ("xT0", "xT1", "tT0", "tT1"):
                    A = name[0] == "x"
                    pe.wait_ge(*(a_split.at(b, 1) if A else c_dve.at(b, C_LO)))
                    ps = B_W[:].bitcast(f16)
                    for s in range(3):
                        if name[2] == "0":
                            nc.tensor.transpose(slot_cols(ps[:, 0:COLS], s), split[:, s, 0:128], id16[:])
                            last = nc.tensor.transpose(slot_cols(ps[:, COLS:2 * COLS], s), lo_main[:, s, :], id16[:])
                        else:
                            last = nc.tensor.transpose(slot_cols(ps[:, 0:COLS], s), split[:, s, 128:256], id16[:])
                    last.then_inc((a_xT_ps if A else c_tT_ps).sem, 1)
                elif name[:2] == "qk":
                    i = int(name[2])
                    pe.wait_ge(*a_xT.at(b, 1))
                    f0 = (i % 2) * 384 + (i // 2) * 128
                    for j in range(3):
                        last = mm(B_W[:, 0:COLS], wqk[:, j // 2, f0:f0 + 128], xT[:, j, :], start=j == 0, stop=j == 2)
                    last.then_inc(a_qk_ps.sem, 1)
                elif name in ("v0", "v1"):
                    for s in ((0, 1) if name == "v0" else (2,)):
                        o = B_W[:, 192 * (s % 2):192 * (s % 2) + 192]
                        for j in range(3):
                            last = mm(o, slot_cols(xT[:, j, :], s), wqk[:, j // 2, 768:960], start=j == 0, stop=j == 2)
                    last.then_inc(a_v_ps.sem, 1)
                elif name in ("pr0", "pr1"):
                    pe.wait_ge(*v_o.at(b, 2))
                    for s in ((0, 1) if name == "pr0" else (2,)):
                        o = B_W[:, 192 * (s % 2):192 * (s % 2) + 192]
                        for j in range(GROUPS):
                            last = mm(o, slot_cols(oT[:, j, :], s), wp[:, j, :], start=j == 0, stop=j == 2)
                    last.then_inc(c_proj_ps.sem, 1)
                elif name == "gate":
                    pe.wait_ge(*c_tT.at(b, 2))
                    t_ = tT[bpar]
                    g0 = TILES * 256
                    for s in range(3):
                        for n, (j, w) in enumerate([(0, w1h0), (1, w1h0), (2, w1hR), (0, w1l0), (3, w1l5)]):
                            last = mm(B_W[:, 16 * s:16 * s + 16], slot_cols(t_[:, j, :], s), w[:, g0:g0 + EXPERTS],
                                      start=n == 0, stop=n == 4)
                    last.then_inc(c_gate_ps.sem, 1)
                elif name == "wT":
                    pe.wait_ge(*c_dve.at(b, C_LO32))
                    plain(pe)
                    for s in range(3):
                        last = nc.tensor.transpose(slot_cols(B_W[0:48, 0:COLS], s), gw[:, s, :], id32[:])
                    last.then_inc(c_wT_ps.sem, 1)

            def body(k, par):
                d, dp = k - 2, par
                for t in range(STEPS):
                    on_d = runs(d)
                    if on_d:
                        if t == 0:
                            pe.wait_ge(*c_tT.at(d, 2))
                            pe.wait_ge(*c_wT.at(d, 1))
                            if isinstance(k, int) and k == 2:
                                pe.wait_ge(w_ready.sem, 9)
                        T = tT[dp]
                        c0 = 768 * (t // 3) + 128 * (t % 3)

                        def products(ps, col):
                            for n, (j, w) in enumerate([(0, w1h0), (1, w1h0), (2, w1hR), (0, w1l0), (3, w1l5)]):
                                last = mm(ps[:, 0:COLS], w[:, col:col + 128], T[:, j, :], start=n == 0, stop=n == 4)
                            return last
                        pe.wait_ge(*d_u.at(d, t - 1))
                        products(B_G, c0).then_inc(d_g_ps.sem, 1)
                    for name, b, sig, i in misc_jobs(k, t):
                        claim_w(k)
                        if name == "difT1":
                            plain(pe)
                        off = 1 if name in ("difT0", "difT1", "sc0", "sc1", "xT0", "xT1", "qk0", "qk1", "qk2", "qk3") else (
                            0 if name in ("v0", "v1", "qk4", "qk5") else -1)
                        misc(k, par, name, b, (par + off) % 2)
                        last_reader[0] = (sig, off, i)
                    if on_d:
                        pe.wait_ge(*d_v.at(d, t - 1))
                        products(B_L, c0 + 384).then_inc(d_l_ps.sem, 1)
                    b3, t3 = (d, t - 3) if t >= 3 else (d - 1, t + 21)
                    if runs(b3):
                        if t3 == 0:
                            pe.wait_ge(*d_sum.at(b3 - 1, 1))
                            for s in range(3):
                                o = (B_Y0, B_Y1)[s // 2][:, 192 * (s % 2):192 * (s % 2) + 192]
                                mm(o, slot_cols(wT32[b3 % 2 if isinstance(b3, int) else dp][32:48, :], s), b2[32:48, :],
                                   start=s != 1, stop=False, skip_group_check=True)
                        pe.wait_ge(*d_act.at(b3, t3))
                        for s in range(3):
                            o = (B_Y0, B_Y1)[s // 2][:, 192 * (s % 2):192 * (s % 2) + 192]
                            last = mm(o, slot_cols(u[t3 % RING][:, :], s), w2[:, t3, :], start=False,
                                      stop=t3 == TILES - 1, skip_group_check=True)
                        last.then_inc(d_y_ps.sem, 1)
                    if on_d:
                        claim_w(k)
                        mm(B_W[:, 0:COLS], sel[:, 128 * t:128 * t + 128], wT16[dp], start=True, stop=True
                           ).then_inc(d_w_ps.sem, 1)
                        last_reader[0] = (d_w, -2, t)
                    if runs(k):
                        h = t // 2
                        r0 = 32 * (h % 4)
                        Q, K = qT[par][r0:r0 + DH, h // 4, :], kT[par][r0:r0 + DH, h // 4, :]
                        pe.wait_ge(*a_qk.at(k, 2 * (h // 4) + 1))
                        pe.wait_ge(*b_y.at(k, t - 1))
                        if t % 2 == 0:
                            for b in range(2):
                                last = mm(B_SC[:, UW * b:UW * b + UW], Q[:, 256 * b:256 * b + 128],
                                          K[:, KEY_COL[b]:KEY_COL[b] + UW], start=True, stop=True)
                        else:
                            for b in range(2):
                                last = mm(B_SC[64 * b:64 * b + 64, 0:UW], Q[:, 128 + 64 * b:192 + 64 * b],
                                          K[:, KEY_COL[b]:KEY_COL[b] + UW], start=True, stop=True)
                        last.then_inc(b_sc_ps.sem, 1)
                    for bv, g, i in v_steps(k, t - 1):
                        vp = (par + (0 if t > 15 else 1)) % 2
                        V = vt[vp]
                        P = pt[i % 2][:].bitcast(bf16)
                        if i == 0:
                            pe.wait_ge(*v_lin.at(bv, g - 1))
                            pe.wait_ge(*a_v_dve.at(bv, 2))
                        pe.wait_ge(*v_pt.at(bv, 4 * g + i))
                        for b in range(2):
                            o = B_AV[32 * i:32 * i + 32, 192 * b:192 * b + 192]
                            mm(o, V[:, b, 4 * g + i, :], P[:, 192 * b:192 * b + 192], start=True, stop=False)
                            last = mm(o, V[:, 2 + b, 4 * g + i, :], P[:, 384:576],
                                      start=False, stop=True)
                        last.then_inc(v_av_ps.sem, 1)
                    for bv, g, i in v_steps(k, t):
                        pp = pat
                        ps = B_PT[:].bitcast(f16)
                        src = pp[:].bitcast(f16)
                        pe.wait_ge(*b_dve.at(bv, NB * g + B_PAT))
                        pe.wait_ge(*v_pt.at(bv, 4 * g + i - 1))
                        main, rest = (0, REST), (128, -PAD)
                        for n in range(2):
                            w0, q0 = (3 * i + n) * UW, 384 + 64 * n
                            nc.tensor.transpose(ps[:, 256 * n:256 * n + 128], src[:, w0 + main[n]:w0 + main[n] + 128],
                                                id16[:])
                            nc.tensor.transpose(ps[64 * n:64 * n + 64, q0:q0 + 128],
                                                src[:, w0 + rest[n]:w0 + rest[n] + 64], id16[:])
                        w0 = (3 * i + 2) * UW
                        nc.tensor.transpose(ps[:, 128:256], src[:, w0 + main[1]:w0 + main[1] + 128], id16[:])
                        nc.tensor.transpose(ps[:, 128:192], src[0:64, w0 + main[0]:w0 + main[0] + 128],
                                            id16[0:64, 0:64])
                        for n in range(2):
                            rows, q0 = slice(64 * n, 64 * n + 64), 512 - 128 * n
                            last = nc.tensor.transpose(ps[rows, q0:q0 + 64], src[rows, w0 + rest[n]:w0 + rest[n] + 64],
                                                       id16[rows, rows])
                        last.then_inc(v_pt_ps.sem, 1)
                if last_reader[0] is not None:
                    sig, off, i = last_reader[0]
                    last_reader[0] = (sig, off - 1, i)

            pe.wait_ge(prep.sem, PREP_DONE)
            pe.wait_ge(prep_act.sem, 1)
            bodies(pe, body)

        @block.scalar
        def _(sc):
            S = nc.scalar

            def body(k, par):
                d, dp = k - 2, par
                for t in range(STEPS):
                    if runs(d):
                        sc.wait_ge(*d_g_ps.at(d, t))
                        sc.wait_ge(*d_y_ps.at(d, t - RING))
                        S.activation(u[t % RING][:], B_G[:, 0:COLS], ACT.Gelu_apprx_sigmoid, scale=1.0 / WSCALE
                                     ).then_inc(d_u.sem, 1)
                    if t == 3 and runs(d - 1):
                        sc.wait_ge(*d_y_ps.at(d - 1, TILES - 1))
                        if not isinstance(d, int) or d - 1 > 0:
                            sc.wait_ge(stored.sem, (d - 1) * 64)
                        S.copy(yo[:, 0:2, :], B_Y0[:, 0:384].rearrange("p (s c) -> p s c", s=2)).then_inc(d_sum.sem, 1)
                        S.copy(yo[:, 2, :], B_Y1[:, 0:192]).then_inc(d_sum.sem, 1)
                    for name, b, _, _ in misc_jobs(k, t):
                        if name == "difT0":
                            sc.wait_ge(*a_difT_ps.at(b, 0))
                            sc.wait_ge(*a_sc_ps.at(b - 1, 1))
                            S.copy(dT[:, 0, :], B_W[:, 0:COLS]).then_inc(a_difT.sem, 1)
                        elif name == "difT1":
                            sc.wait_ge(*a_difT_ps.at(b, 1))
                            S.copy(dT[0:64, 1, :], B_W[0:64, 0:COLS]).then_inc(a_difT.sem, 1)
                        elif name in ("sc0", "sc1"):
                            i = int(name[2])
                            sc.wait_ge(*a_sc_ps.at(b, i))
                            sc.wait_ge(*a_dve.at(b - 1, A_HD))
                            sc.wait_ge(*c_res.at(b - 3))
                            n = 2 - i
                            S.activation(th[:, 2 * i:2 * i + n, :],
                                         B_W[:, 0:192 * n].rearrange("p (s c) -> p s c", s=n), ACT.Tanh, scale=0.5
                                         ).then_inc(a_tanh.sem, 1)
                        elif name in ("xT0", "xT1"):
                            i = int(name[2])
                            sc.wait_ge(*a_xT_ps.at(b, i))
                            if i == 0:
                                sc.wait_ge(*a_qk_ps.at(b - 1, 5))
                            n = 2 - i
                            S.copy(xT[:, 2 * i:2 * i + n, :].bitcast(f32), B_W[:, 0:192 * n].rearrange(
                                "p (s c) -> p s c", s=n)).then_inc(a_xT.sem, 1)
                        elif name[:2] == "qk":
                            i = int(name[2])
                            sc.wait_ge(*a_qk_ps.at(b, i))
                            sc.wait_ge(*a_qk_rnd.at(b, i - 1))
                            c = (i % 2) * 3 + i // 2
                            S.activation(qf[:], B_W[:, 0:COLS], ACT.Identity, scale=qscale[:, c:c + 1],
                                         bias=qbias[:, c:c + 1]).then_inc(a_qk_lin.sem, 1)
                        elif name in ("v0", "v1", "pr0", "pr1"):
                            i = int(name[-1])
                            if name[0] == "v":
                                sc.wait_ge(*a_v_ps.at(b, i))
                                sc.wait_ge(*c_dve.at(b - 2, C_LO))
                            else:
                                sc.wait_ge(*c_proj_ps.at(b, i))
                                if runs(k):
                                    sc.wait_ge(*a_v_dve.at(k, 2))
                            n = 2 - i
                            S.copy(pf[:, 2 * i:2 * i + n, :], B_W[:, 0:192 * n].rearrange("p (s c) -> p s c", s=n)
                                   ).then_inc((a_v_act if name[0] == "v" else c_proj).sem, 1)
                        elif name == "gate":
                            sc.wait_ge(*c_gate_ps.at(b))
                            S.activation(g20[:, :, 0:EXPERTS], B_W[:, 0:48].rearrange("p (s e) -> p s e", s=3), ACT.Copy,
                                         scale=1.0 / WSCALE).then_inc(c_gate.sem, 1)
                        elif name == "tT0":
                            sc.wait_ge(*c_tT_ps.at(b, 0))
                            cp = (par + 1) % 2
                            S.copy(tT[cp][:, 0:2, :].bitcast(f32), B_W[:, 0:384].rearrange("p (s c) -> p s c", s=2)
                                   ).then_inc(c_tT.sem, 1)
                        elif name == "tT1":
                            sc.wait_ge(*c_tT_ps.at(b, 1))
                            cp = (par + 1) % 2
                            S.copy(tT[cp][:, 2, :].bitcast(f32), B_W[:, 0:192]).then_inc(c_tT.sem, 1)
                            S.copy(tT[cp][0:64, 3, :].bitcast(f32), B_W[0:64, 0:192]).then_inc(c_tT.sem, 1)
                        elif name == "wT":
                            sc.wait_ge(*c_wT_ps.at(b))
                            cp = (par + 1) % 2
                            S.copy(wT16[cp], B_W[0:32, 0:COLS]).then_inc(c_wT.sem, 1)
                            S.copy(wT32[cp][32:48, :], B_W[32:48, 0:COLS]).then_inc(c_wT.sem, 1)
                    if runs(d):
                        sc.wait_ge(*d_l_ps.at(d, t))
                        sc.wait_ge(*d_act.at(d, t - LRING))
                        S.activation(lin[t % LRING][:], B_L[:, 0:COLS], ACT.Relu, bias=lift[:]).then_inc(d_v.sem, 1)
                    for b, g, s in b_steps(k, t):
                        if s == 1:
                            sc.wait_ge(*b_dve.at(b, NB * g + B_NEG))
                            sc16 = ai[(g + (par if t >= 8 else par + 1)) % 2]
                            for i in range(UNITS - SHARE, UNITS):
                                last = S.activation(sc16[:, i, :], sc16[:, i, :], ACT.Identity, bias=nmax[:, i:i + 1])
                            last.then_inc(b_sub.sem, 1)
                        if s == 5:
                            sc.wait_ge(*b_dve.at(b, NB * g + B_RS4))
                            for i in range(UNITS - SHARE, UNITS):
                                last = S.activation(ee[:, i, :], ee[:, i, :], ACT.Copy, scale=rs4[:, i:i + 1])
                            last.then_inc(b_t4_act.sem, 1)
                        if s == 3:
                            sc.wait_ge(*b_dve.at(b, NB * g + B_R))
                            S.activation(ee[:], xq[:], ACT.Square, bias=cc(HB)).then_inc(b_sq.sem, 1)
                    if t == 3 and runs(k - 1):
                        sc.wait_ge(*a_dve.at(k - 1, A_H))
                        sc.wait_ge(*c_dve.at(k - 2, C_H2))
                        S.copy(hres[:], h1[(par + 1) % 2][:]).then_inc(a_keep.sem, 1)
                    if runs(d):
                        sc.wait_ge(*d_w_ps.at(d, t))
                        S.copy(wb[t % LRING][:], B_W[:, 0:COLS]).then_inc(d_w.sem, 1)
                    if runs(k):
                        i = (t % 8) // 2 * 3
                        g = t // 8
                        yb = ai[(g + par) % 2]
                        sc.wait_ge(*b_sc_ps.at(k, t))
                        if t % 8 == 0:
                            sc.wait_ge(*b_dve.at(k, NB * (g - 2) + B_R))
                        if t % 2 == 0:
                            S.activation(yb[:, i:i + 2, :], B_SC[:, 0:2 * UW].rearrange("p (u n) -> p u n", u=2),
                                         ACT.Identity, scale=cc(KAPPA), bias=hmagic[:]).then_inc(b_y.sem, 1)
                        else:
                            S.activation(yb[:, i + 2, :], B_SC[:, 0:UW], ACT.Identity, scale=cc(KAPPA), bias=hmagic[:]
                                         ).then_inc(b_y.sem, 1)
                    for bv, g, i in v_steps(k, t):
                        sc.wait_ge(*v_pt_ps.at(bv, 4 * g + i))
                        sc.wait_ge(*v_av_ps.at(bv, 4 * g + i - 2))
                        S.copy(pt[i % 2][:], B_PT[:, 0:288]).then_inc(v_pt.sem, 1)
                    for bv, g, i in v_steps(k, t - 1):
                        if i == 3:
                            sc.wait_ge(*v_av_ps.at(bv, 4 * g + 3))
                            sc.wait_ge(*v_rnd.at(bv, g - 1))
                            S.activation(of[:], B_AV[:, 0:COLS], ACT.Identity, scale=cc(KO), bias=magic[:]
                                         ).then_inc(v_lin.sem, 1)
                    if t == 21 and runs(k - 1):
                        sc.wait_ge(*c_dve.at(k - 1, C_D))
                        S.activation(gt[:], gd[:], ACT.Tanh, scale=0.5).then_inc(c_tanh.sem, 1)

            sc.wait_ge(prep.sem, PREP_DONE)
            S.copy(consts[:, 31:32], magic[:]).then_inc(prep_act.sem, 1)

            def with_weights(k, par):
                if isinstance(k, int) and k == 0:
                    for c in range(9):
                        n = 768 if c < 8 else EXPERTS
                        sc.wait_ge(w_high.sem, c + 1)
                        S.copy(w1h0[:, 768 * c:768 * c + n], wtmp[0][:, 0:n])
                        S.copy(w1hR[:, 768 * c:768 * c + n], wtmp[1][:, 0:n]).then_inc(prep_act.sem, 1)
                    sc.wait_ge(w_ready.sem, 9)
                body(k, par)

            bodies(sc, with_weights)

        @block.gpsimd
        def _(pool):
            G = nc.gpsimd

            def tile(b, t, par):
                pool.wait_ge(*d_p.at(b, t))
                G.tensor_tensor(u[t % RING][:], u[t % RING][:], lin[t % LRING][:], ALU.mult).then_inc(d_half.sem, 1)
                pool.wait_ge(*d_half.at(b, t))
                pool.wait_ge(*d_w.at(b, t))
                G.tensor_tensor(u[t % RING][:], u[t % RING][:], wb[t % LRING][:], ALU.mult).then_inc(d_act.sem, 1)

            def differences(b):
                pool.wait_ge(x_loaded.sem, (b + 1) * 64)
                pool.wait_ge(*a_dve.at(b - 1, A_HD))
                pool.wait_ge(*a_difT_ps.at(b - 1, 1))
                G.tensor_tensor(dif[:], x[:, :, 0:C], x[:, :, C:2 * C], ALU.subtract).then_inc(a_dif.sem, 1)

            def body(k, par):
                for t in range(STEPS):
                    for b, g, s in b_steps(k, t):
                        if s == 5:
                            pool.wait_ge(*b_dve.at(b, NB * g + B_RS4))
                            plain(pool)
                            for i in range(UNITS - SHARE):
                                last = G.tensor_scalar(ee[:, i, :], ee[:, i, :], rs4[:, i:i + 1], 1.0, ALU.mult, ALU.mult)
                            last.then_inc(b_t4.sem, 1)
                    if t == 0 and runs(k - 3):
                        tile(k - 3, TILES - 1, par)
                    if t >= 1 and runs(k - 2):
                        tile(k - 2, t - 1, par)
                    if t == 20 and runs(k + 2):
                        differences(k + 2)
                    if t == 4 and runs(k - 3):
                        pool.wait_ge(*d_sum.at(k - 3, 1))
                        pool.wait_ge(*c_res.at(k - 3))
                        G.tensor_tensor(yo[:], yo[:], res[(par + 1) % 2][:], ALU.add).then_inc(d_out.sem, 1)
                    if t == 6 and runs(k):
                        def row(j):
                            return vrow[:, j, :].unsqueeze(1).to_broadcast([128, 3, C])
                        pool.wait_ge(*a_v_act.at(k, 1))
                        G.tensor_tensor(vf[:], vf[:], row(0), ALU.mult).then_inc(a_v_lin.sem, 1)
                        pool.wait_ge(*a_v_lin.at(k, 0))
                        G.tensor_tensor(vf[:], vf[:], row(1), ALU.add).then_inc(a_v_lin.sem, 1)
                    if t == 17 and runs(k - 1):
                        pool.wait_ge(*c_dve.at(k - 1, C_XN))
                        G.tensor_tensor(res[(par + 1) % 2][:], h2[:], cn[:], ALU.add).then_inc(c_res.sem, 1)
                    if t == 7 and runs(k + 1):
                        pool.wait_ge(*a_dve.at(k + 1, A_VAR))
                        pool.wait_ge(*a_dve.at(k, A_XN))
                        G.tensor_tensor(rstd[:, 0:3], vare[:, 0:3], negh[:, 0:3], ALU.pow).then_inc(a_rstd.sem, 1)
                    if t == 16 and runs(k - 1):
                        pool.wait_ge(*c_dve.at(k - 1, C_VAR))
                        G.tensor_tensor(crstd[:, 0:3], cvar[:, 0:3], negh[:, 0:3], ALU.pow).then_inc(c_rstd.sem, 1)
                        pool.wait_ge(*c_rstd.at(k - 1, 0))
                        G.tensor_tensor(cvar2[:, 0:3], crstd[:, 0:3], crstd[:, 0:3], ALU.mult).then_inc(c_rstd.sem, 1)
                        pool.wait_ge(*c_rstd.at(k - 1, 1))
                        plain(pool)
                        G.tensor_scalar(cvar2[:, 0:3], cvar2[:, 0:3], -EPS, 1.0 + EPS, ALU.mult, ALU.add
                                        ).then_inc(c_rstd.sem, 1)
                        pool.wait_ge(*c_rstd.at(k - 1, 2))
                        G.tensor_tensor(crstd2[:, 0:3], cvar2[:, 0:3], negh[:, 0:3], ALU.pow).then_inc(c_rstd.sem, 1)

            pool.wait_ge(prep.sem, PREP_DONE)
            differences(0)
            bodies(pool, body)

        @block.vector
        def _(ve):
            V = nc.vector
            n_prep = [0]

            def step(ins):
                n_prep[0] += 1
                ins.then_inc(prep.sem, 1)
                ve.wait_ge(prep.sem, n_prep[0])

            for tl in (x, *h1, dT, xT, qT[0], qT[1], kT[0], kT[1], vt[0], vt[1], pat, tT[0], tT[1],
                       res[0], res[1], hres, gs, vare, rstd, cvar, crstd, cvar2, crstd2):
                V.memset(tl[:], 0.0)
            step(V.memset(magic[:], MAGIC))
            for tl in (tT[0], tT[1]):
                V.memset(tl[64:65, 3, :], 1.0)
                V.memset(tl[96:97, 3, :], 1.0)
            V.memset(g20[:], BIG)
            V.memset(rep8[:], BIG)
            V.memset(hmagic[:], HMAGIC)
            V.memset(lift[:], (LIMIT - 1.0) * WSCALE)
            step(V.memset(negh[:], -0.5))
            ve.wait_ge(ld_const.sem, 16 * N_CONST)
            step(V.reciprocal(iscal[:], scal[:]))
            s1, sa, s2, s3 = (scal[:, i:i + 1] for i in range(4))
            i1, ia, i2, i3 = (iscal[:, i:i + 1] for i in range(4))
            tmp, tmq, tmr, xf0, bf_, cf = (cc(i) for i in range(10, 16))

            def ts(out, in0, sc1, sc2, op0, op1=ALU.bypass):
                if op1 == ALU.bypass:
                    return V.tensor_scalar(out, in0, sc1, None, op0)
                return V.tensor_scalar(out, in0, sc1, sc2, op0, op1)

            def floor(out, src):
                step(ts(tmq, src, MAGIC, MAGIC, ALU.add, ALU.subtract))
                step(V.tensor_tensor(tmr, tmq, src, ALU.is_gt))
                step(V.tensor_tensor(out, tmq, tmr, ALU.subtract))

            step(ts(tmp, s1, s1, 0.25, ALU.mult, ALU.mult))
            step(V.tensor_tensor(cc(KAPPA), tmp, ia, ALU.mult))
            step(ts(tmp, ia, -0.6931, None, ALU.mult))
            floor(xf0, tmp)
            step(ts(cc(KX), xf0, -1.0, None, ALU.mult))
            step(ts(cc(CLAMP), xf0, 30.0, None, ALU.mult))
            step(V.reciprocal(tmp, cc(KX)))
            step(ts(cc(NINVX), tmp, -1.0, None, ALU.mult))
            step(ts(cc(Q1OFF), tmp, 0.5, HMAGIC - 0.5, ALU.mult, ALU.add))
            step(ts(tmp, ia, 0.96963238 / 0.35815147, None, ALU.mult))
            floor(bf_, tmp)
            step(ts(tmp, ia, ia, 1.0 / 0.35815147, ALU.mult, ALU.mult))
            floor(cf, tmp)
            step(ts(cc(HB), bf_, 0.5, None, ALU.mult))
            step(V.tensor_tensor(tmp, cc(HB), cc(HB), ALU.mult))
            step(V.tensor_tensor(cc(CP), cf, tmp, ALU.subtract))
            step(ts(tmp, cf, 1.0, 2.0**47, ALU.min, ALU.mult))
            step(ts(cc(KO), tmp, s1, i2, ALU.mult, ALU.mult))
            step(ts(qscale[:], qscale[:], i1, None, ALU.mult))
            step(ts(qbias[:], qbias[:], i1, None, ALU.mult))
            step(ts(vrow[:], vrow[:], i1, None, ALU.mult))
            pr = flat16[1][:].bitcast(f32)[:, 576:768]
            step(V.reciprocal(pr, prow[:, 0, :]))
            step(ts(prow[:, 0, :], prow[:, 0, :], s2, i3, ALU.mult, ALU.mult))
            step(ts(prow[:, 1, :], prow[:, 1, :], i3, None, ALU.mult))
            yw = ee[:].rearrange("p u n -> p (u n)")[:, 0:1920].rearrange("p (t f) -> p t f", t=2)
            ys = flat16[0][:].bitcast(f32)[:, 0:960]
            step(V.reciprocal(ys, ys))
            for t_ in range(2):
                step(V.tensor_tensor(yw[:, t_, :], yw[:, t_, :], ys, ALU.mult))
            step(ts(yw, yw, MAGIC, MAGIC, ALU.add, ALU.subtract))
            step(ts(wqk[:], yw, 127.0, -128.0, ALU.min, ALU.max))
            ew = flat16[1][:].bitcast(f32)[:, 0:576].rearrange("p (t f) -> p t f", t=3)
            for t_ in range(3):
                step(V.tensor_tensor(ew[:, t_, :], ew[:, t_, :], pr, ALU.mult))
            step(ts(ew, ew, MAGIC, MAGIC, ALU.add, ALU.subtract))
            step(ts(wp[:], ew, 127.0, -128.0, ALU.min, ALU.max))
            step(V.memset(bst[64:128, :], 0.0))
            assert n_prep[0] == PREP_DONE, n_prep[0]

            def norm(b, src, stt, agg, base_sig, i_stat, i_agg):
                for s in range(3):
                    last = V.bn_stats(stt[:, s, 0:6], src[:, s, :])
                last.then_inc(base_sig.sem, 1)
                ve.wait_ge(*base_sig.at(b, i_stat))
                plain(ve)
                for s in range(3):
                    last = V.bn_aggr(agg[:, s, :], stt[:, s, 0:6])
                last.then_inc(base_sig.sem, 1)
                ve.wait_ge(*base_sig.at(b, i_agg))

            def stage_a_pool(b, par, hp):
                ve.wait_ge(*a_tanh.at(b, 1))
                V.scalar_tensor_tensor(th[:], th[:], 1.0, dif[:], ALU.add, ALU.mult).then_inc(a_dve.sem, 1)
                ve.wait_ge(*a_dve.at(b, A_HD))
                ve.wait_ge(*a_keep.at(b - 2))
                V.scalar_tensor_tensor(h1[hp][:], th[:], 0.5, x[:, :, C:2 * C], ALU.mult, ALU.add
                                       ).then_inc(a_dve.sem, 1)
                ve.wait_ge(*a_dve.at(b, A_H))
                norm(b, h1[hp], stats, mv, a_dve, A_STAT, A_AGG)
                ts(vare[:, 0:3], mv[:, :, 1], EPS, None, ALU.add).then_inc(a_dve.sem, 1)

            def stage_a_split(b, hp):
                ve.wait_ge(*a_rstd.at(b))
                ve.wait_ge(*c_tT_ps.at(b - 3, 1))
                for s in range(3):
                    last = ts(xn[:, s, :], h1[hp][:, s, :], mv[:, s, 0:1], rstd[:, s:s + 1], ALU.subtract, ALU.mult)
                last.then_inc(a_dve.sem, 1)
                ve.wait_ge(*a_dve.at(b, A_XN))
                V.tensor_copy(hi, xn[:]).then_inc(a_split.sem, 1)
                ve.wait_ge(*a_split.at(b, 0))
                V.tensor_tensor(lo_rest, xn[:, :, 128:C], hi[:, :, 128:C], ALU.subtract)
                V.tensor_tensor(lo_main, xn[:, :, 0:128], hi[:, :, 0:128], ALU.subtract).then_inc(a_split.sem, 1)

            def round_qk(b, par, i):
                dst = (qT, kT)[i % 2][par][:, i // 2, :]
                ve.wait_ge(*a_qk.at(b, i - 1))
                ve.wait_ge(*a_qk_lin.at(b, i))
                ts(qr[:], qf[:], MAGIC, MAGIC, ALU.add, ALU.subtract).then_inc(a_qk_rnd.sem, 1)
                ve.wait_ge(*a_qk_rnd.at(b, i))
                if i < 2:
                    ve.wait_ge(*b_sc_ps.at(b - 2, 23))
                ts(dst, qr[:], 127.0, -128.0, ALU.min, ALU.max).then_inc(a_qk.sem, 1)

            def values(b, par):
                ve.wait_ge(*a_v_lin.at(b, 1))
                ve.wait_ge(*v_av_ps.at(b - 2, 11))
                ts(vf[:], vf[:], MAGIC, MAGIC, ALU.add, ALU.subtract).then_inc(a_v_dve.sem, 1)
                ve.wait_ge(*a_v_dve.at(b, 0))
                ts(vf[:], vf[:], 127.0, -128.0, ALU.min, ALU.max).then_inc(a_v_dve.sem, 1)
                ve.wait_ge(*a_v_dve.at(b, 1))
                heads = vf[:].rearrange("p s (h e) -> p s h e", e=DH)
                ts(vt[par][:, 0:2, :, 0:DH], heads[:, 0:2], 2.0**64, None, ALU.mult)
                for m in range(2):
                    last = ts(vt[par][:, 2 + m, :, 0:DH], heads[:, 2], vmask[:, m:m + 1], None, ALU.mult)
                last.then_inc(a_v_dve.sem, 1)

            def softmax_part(b, g, s, par):
                sc16, pp = ai[(g + par) % 2], pat
                sem = b_dve.sem
                if s == 0:
                    ve.wait_ge(*b_y.at(b, 8 * g + 7))
                    ts(sc16[:], sc16[:], HMAGIC, -128.0, ALU.subtract, ALU.max).then_inc(sem, 1)
                    ve.wait_ge(*b_dve.at(b, NB * g + B_CLIP))
                    V.tensor_tensor(q1[:, :, 0:HALF], sc16[:, :, 0:HALF], sc16[:, :, UW - HALF:UW], ALU.max
                                    ).then_inc(sem, 1)
                    ve.wait_ge(*b_dve.at(b, NB * g + B_HALF))
                    V.tensor_reduce(rmax[:], q1[:, :, 0:HALF], AX.X, ALU.max).then_inc(sem, 1)
                    ve.wait_ge(*b_dve.at(b, NB * g + B_MAX))
                    ts(nmax[:], rmax[:], 127.0, -1.0, ALU.min, ALU.mult).then_inc(sem, 1)
                elif s == 1:
                    n = UNITS - SHARE
                    ve.wait_ge(*b_dve.at(b, NB * g + B_NEG))
                    V.tensor_tensor(sc16[:, 0:n, :], sc16[:, 0:n, :], nmax[:, 0:n].unsqueeze(2).to_broadcast([128, n, UW]),
                                    ALU.add).then_inc(sem, 1)
                elif s == 2:
                    ve.wait_ge(*b_dve.at(b, NB * g + B_SUB))
                    ve.wait_ge(*b_sub.at(b, g))
                    ts(sc16[:], sc16[:], 0.0, cc(CLAMP), ALU.min, ALU.max).then_inc(sem, 1)
                    ve.wait_ge(*b_dve.at(b, NB * g + B_CLAMP))
                    ts(q1[:], sc16[:], cc(NINVX), cc(Q1OFF), ALU.mult, ALU.add).then_inc(sem, 1)
                    ve.wait_ge(*b_dve.at(b, NB * g + B_Q1))
                    ts(xq[:], q1[:], HMAGIC, cc(KX), ALU.subtract, ALU.mult).then_inc(sem, 1)
                    ve.wait_ge(*b_dve.at(b, NB * g + B_XQ))
                    ts(q1[:].bitcast(i16), q1[:], -128.0, (HMAGIC + 127.0) * 128.0, ALU.mult, ALU.add).then_inc(sem, 1)
                    ve.wait_ge(*b_dve.at(b, NB * g + B_P2))
                    V.tensor_tensor(xq[:], sc16[:], xq[:], ALU.add).then_inc(sem, 1)
                elif s == 4:
                    ve.wait_ge(*b_sq.at(b, g))
                    V.scalar_tensor_tensor(ee[:], ee[:], cc(CP), q1[:].bitcast(bf16), ALU.add, ALU.mult).then_inc(sem, 1)
                    ve.wait_ge(*b_dve.at(b, NB * g + B_E))
                    V.tensor_reduce(rsum[:], ee[:], AX.X, ALU.add).then_inc(sem, 1)
                    ve.wait_ge(*b_dve.at(b, NB * g + B_S))
                    ts(rsum[:], rsum[:], 0.25, None, ALU.mult).then_inc(sem, 1)
                    ve.wait_ge(*b_dve.at(b, NB * g + B_S4))
                    V.reciprocal(rs4[:], rsum[:]).then_inc(sem, 1)
                elif s == 6:
                    ve.wait_ge(*b_t4.at(b, g))
                    ve.wait_ge(*b_t4_act.at(b, g))
                    hi = ee[:].rearrange("p u n -> p (u n)").bitcast(u16).rearrange("p (n w) -> p n w", w=2)[:, :, 1]
                    ts(f4.rearrange("p u n -> p (u n)"), hi, 0x3F80, 0, ALU.bitwise_and, ALU.bitwise_or).then_inc(sem, 1)
                    ve.wait_ge(*b_dve.at(b, NB * g + B_F4))
                    V.scalar_tensor_tensor(ee[:], f4.bitcast(bf16), 6.0, ee[:], ALU.subtract, ALU.mult).then_inc(sem, 1)
                    ve.wait_ge(*b_dve.at(b, NB * g + B_T6))
                elif s == 7:
                    ve.wait_ge(*v_pt_ps.at(b, 4 * (g - 1) + 3))
                    hi = ee[:].rearrange("p u n -> p (u n)").bitcast(u16).rearrange("p (n w) -> p n w", w=2)[:, :, 1]
                    ts(pp[:, 0:GW].bitcast(u16), hi, 0x7F80, 0, ALU.bitwise_and, ALU.bitwise_or).then_inc(sem, 1)
                    ve.wait_ge(*b_dve.at(b, NB * g + B_MASK))
                    ts(pp[:, 0:GW], pp[:, 0:GW], 115.0 * 128.0, 0.0, ALU.subtract, ALU.max).then_inc(sem, NB - 17)

            def attention_out(b, g):
                ve.wait_ge(*v_o.at(b, g - 1))
                ve.wait_ge(*v_lin.at(b, g))
                ts(orr[:], of[:], MAGIC, -128.0, ALU.subtract, ALU.max).then_inc(v_rnd.sem, 1)
                ve.wait_ge(*v_rnd.at(b, g))
                if g == 0:
                    ve.wait_ge(*c_proj_ps.at(b - 1, 1))
                ts(oT[:, g, :], orr[:], 127.0, None, ALU.min).then_inc(v_o.sem, 1)

            def c_residual(b):
                sem = c_dve.sem
                ve.wait_ge(*a_keep.at(b))
                ve.wait_ge(*c_proj.at(b, 1))
                V.tensor_tensor(pf[:], pf[:], prow[:, 0, :].unsqueeze(1).to_broadcast([128, 3, C]), ALU.mult).then_inc(sem, 1)
                ve.wait_ge(*c_dve.at(b, C_SCALE))
                V.tensor_tensor(pf[:], pf[:], prow[:, 1, :].unsqueeze(1).to_broadcast([128, 3, C]), ALU.add).then_inc(sem, 1)
                ve.wait_ge(*c_dve.at(b, C_BIAS))
                ts(pf[:], pf[:], MAGIC, MAGIC, ALU.add, ALU.subtract).then_inc(sem, 1)
                ve.wait_ge(*c_dve.at(b, C_RND))
                ts(pf[:], pf[:], 127.0, -128.0, ALU.min, ALU.max).then_inc(sem, 1)
                ve.wait_ge(*c_dve.at(b, C_CLIP))
                ve.wait_ge(*c_res.at(b - 1))
                V.scalar_tensor_tensor(h2[:], pf[:], s3, hres[:], ALU.mult, ALU.add).then_inc(sem, 1)
                ve.wait_ge(*c_dve.at(b, C_H2))
                norm(b, h2, cstats, cmv, c_dve, C_STAT, C_AGG)
                ts(cvar[:, 0:3], cmv[:, :, 1], EPS, None, ALU.add).then_inc(sem, 1)

            def c_split(b, rp):
                sem = c_dve.sem
                if not isinstance(b, int) or b + 2 < BLOCKS:
                    ve.wait_ge(*a_xT_ps.at(b + 2, 1))
                ve.wait_ge(*c_rstd.at(b, 0))
                for s in range(3):
                    last = ts(cn[:, s, :], h2[:, s, :], cmv[:, s, 0:1], crstd[:, s:s + 1], ALU.subtract, ALU.mult)
                last.then_inc(sem, 1)
                ve.wait_ge(*c_dve.at(b, C_XN))
                ve.wait_ge(*c_rstd.at(b, 3))
                for s in range(3):
                    last = ts(ct[:, s, :], cn[:, s, :], crstd2[:, s:s + 1], None, ALU.mult)
                last.then_inc(sem, 1)
                ve.wait_ge(*c_dve.at(b, C_T))
                V.tensor_copy(hi, ct[:]).then_inc(sem, 1)
                ve.wait_ge(*c_dve.at(b, C_HI))
                V.tensor_tensor(lo_rest, ct[:, :, 128:C], hi[:, :, 128:C], ALU.subtract)
                V.tensor_tensor(lo_main, ct[:, :, 0:128], hi[:, :, 0:128], ALU.subtract).then_inc(sem, 1)

            def c_top(b):
                sem = c_dve.sem
                ve.wait_ge(*c_gate.at(b))
                plain(ve)
                for s in range(3):
                    last = V.max(top8[:, s, :], g20[:, s, 0:EXPERTS])
                last.then_inc(sem, 1)
                ve.wait_ge(*c_dve.at(b, C_TOP))
                V.tensor_copy(rep8[:, :, 0:TOPK], top8[:, :, 0:TOPK]).then_inc(sem, 1)
                ve.wait_ge(*c_dve.at(b, C_REP))
                plain(ve)
                for s in range(3):
                    last = V.match_replace(gz[:, s, :], rep8[:, s, :], g20[:, s, :], -BIG)
                last.then_inc(sem, 1)
                ve.wait_ge(*c_dve.at(b, C_MR))
                V.tensor_tensor(gm[:], gz[:, :, 0:EXPERTS], g20[:, :, 0:EXPERTS], ALU.is_lt).then_inc(sem, 1)
                V.tensor_tensor(gd[:], g20[:, :, 0:EXPERTS], top8[:, :, 0:1].to_broadcast([128, 3, EXPERTS]), ALU.subtract
                                ).then_inc(sem, 1)

            def c_weights(b):
                sem = c_dve.sem
                ve.wait_ge(*c_tanh.at(b))
                ts(gn[:], gt[:], 1.0, None, ALU.add).then_inc(sem, 1)
                ts(gr[:], gt[:], -1.0, 1.0, ALU.mult, ALU.add).then_inc(sem, 1)
                ve.wait_ge(*c_dve.at(b, C_DEN))
                V.reciprocal(gr[:], gr[:]).then_inc(sem, 1)
                ve.wait_ge(*c_dve.at(b, C_RCP))
                V.tensor_tensor(gn[:], gn[:], gr[:], ALU.mult).then_inc(sem, 1)
                ve.wait_ge(*c_dve.at(b, C_E1))
                V.tensor_tensor(gn[:], gn[:], gm[:], ALU.mult).then_inc(sem, 1)
                ve.wait_ge(*c_dve.at(b, C_E2))
                V.tensor_reduce(gs[:, 0:3], gn[:], AX.X, ALU.add).then_inc(sem, 1)
                ve.wait_ge(*c_dve.at(b, C_SUM))
                V.reciprocal(gsr[:, 0:3], gs[:, 0:3]).then_inc(sem, 1)
                ve.wait_ge(*c_dve.at(b, C_SR))
                V.tensor_tensor(gw[:, :, 32:48], gn[:], gsr[:, 0:3].unsqueeze(2).to_broadcast([128, 3, EXPERTS]), ALU.mult
                                ).then_inc(sem, 1)
                ve.wait_ge(*c_dve.at(b, C_W))
                V.tensor_copy(gh16[:], gw[:, :, 32:48]).then_inc(sem, 1)
                ve.wait_ge(*c_dve.at(b, C_H16))
                V.tensor_copy(gw[:, :, 0:16], gh16[:]).then_inc(sem, 1)
                V.tensor_tensor(gw[:, :, 16:32], gw[:, :, 32:48], gh16[:], ALU.subtract).then_inc(sem, 1 + NC_ - 28)

            def tile(b, t):
                ve.wait_ge(*d_v.at(b, t))
                ts(lin[t % LRING][:], lin[t % LRING][:], 2.0 * LIMIT * WSCALE, (1.0 - LIMIT) * WSCALE, ALU.min, ALU.add)
                ts(u[t % RING][:], u[t % RING][:], GLU_MAX, None, ALU.min).then_inc(d_p.sem, 1)

            def split_weights():
                for c in range(9):
                    n = 768 if c < 8 else EXPERTS
                    cs = slice(768 * c, 768 * c + n)
                    ve.wait_ge(w_loaded.sem, 48 * (c + 1))
                    if c:
                        ve.wait_ge(w_ready.sem, c)
                    for i in range(2):
                        ts(wtmp[i][:, 0:n], wst[:, i, 0:n], lnscale[:, i:i + 1], WSCALE, ALU.mult, ALU.mult)
                    if c < 8:
                        ts(bs[64:128, 0:384], bst[64:128, 0:384], WSCALE, None, ALU.mult)
                        last = ts(bs[64:128, 384:768], bst[64:128, 384:768], 1.0, WSCALE, ALU.add, ALU.mult)
                    else:
                        last = ts(bs[64:128, 0:n], bst[64:128, 0:n], WSCALE, None, ALU.mult)
                    last.then_inc(w_high.sem, 1)
                    ve.wait_ge(w_high.sem, c + 1)
                    V.tensor_copy(w1l5[64:96, cs], bs[64:96, 0:n])
                    V.tensor_copy(bh[96:128, 0:n], bs[96:128, 0:n]).then_inc(w_split.sem, 1)
                    ve.wait_ge(w_split.sem, c + 1)
                    ve.wait_ge(prep_act.sem, c + 2)
                    V.tensor_tensor(w1l5[96:128, cs], bs[96:128, 0:n], bh[96:128, 0:n], ALU.subtract)
                    V.tensor_tensor(w1l0[:, cs], wtmp[0][:, 0:n], w1h0[:, cs], ALU.subtract)
                    V.tensor_tensor(w1l5[0:64, cs], wtmp[1][0:64, 0:n], w1hR[0:64, cs], ALU.subtract
                                    ).then_inc(w_ready.sem, 1)

            def body(k, par):
                if isinstance(k, int) and k == 0:
                    split_weights()
                d, dp = k - 2, par
                for t in range(STEPS):
                    if t == 0 and runs(d - 1):
                        tile(d - 1, TILES - 1)
                    if t >= 1 and runs(d):
                        tile(d, t - 1)
                    if t == 5 and runs(k + 1):
                        stage_a_pool(k + 1, (par + 1) % 2, (par + 1) % 2)
                    if t == 8 and runs(k + 1):
                        stage_a_split(k + 1, (par + 1) % 2)
                    if t in (13, 16, 18, 23) and runs(k + 1):
                        round_qk(k + 1, (par + 1) % 2, (13, 16, 18, 23).index(t))
                    if t in (7, 9) and runs(k):
                        round_qk(k, par, 4 + t // 9)
                    if t == 7 and runs(k):
                        values(k, par)
                    if t == 21 and runs(k):
                        attention_out(k, 0)
                    if t in (5, 13) and runs(k - 1):
                        attention_out(k - 1, 1 + t // 13)
                    if runs(k - 1):
                        if t == 15:
                            c_residual(k - 1)
                        if t == 17:
                            c_split(k - 1, (par + 1) % 2)
                        if t == 21:
                            c_top(k - 1)
                        if t == 22:
                            c_weights(k - 1)
                    for b, g, s in b_steps(k, t):
                        softmax_part(b, g, s, par if t >= 8 else (par + 1) % 2)

            bodies(ve, body)


def constants():
    sel = np.zeros((32, TILES, 128), np.float16)
    for pair in range(EXPERTS // 2):
        for j in range(3):
            for half in range(2):
                e = 2 * pair + (j if j < 2 else half)
                for part in (0, EXPERTS):
                    sel[part + e, 3 * pair + j, 64 * half:64 * half + 64] = 1.0 / WSCALE
    vmask = np.zeros((128, 2), np.float32)
    for b, (first, end) in enumerate(REST_ROWS):
        vmask[first:end, b] = 2.0**64
    return {"vmask": vmask, "id16": np.eye(128, dtype=np.float16), "id32": np.eye(128, dtype=np.float32),
            "sel": sel.reshape(32, TILES * 128)}


def expert_columns(w):
    halves = w.reshape(*w.shape[:-2], EXPERTS // 2, 2, 2, C)
    main = np.moveaxis(halves[..., 0:128], -3, -2)
    rest = np.moveaxis(halves[..., 128:C], -3, -2)
    main = main.reshape(*main.shape[:-2], 256)
    rest = rest.reshape(*rest.shape[:-2], 128)
    out = np.concatenate([main, rest], axis=-1)
    return out.reshape(*w.shape[:-2], EXPERTS * 384)


def rows_128_64(w):
    return np.stack([w[0:128], np.concatenate([w[128:192], w[128:192]])], axis=1)


def pad_heads(w):
    z = np.zeros((HEADS, 32) + w.shape[1:], w.dtype)
    z[:, 0:DH] = w.reshape((HEADS, DH) + w.shape[1:])
    return z.reshape((HEADS * 32,) + w.shape[1:])


def kernel(**inputs):
    import concourse.bacc as bacc
    from concourse.bass_utils import run_bass_kernel_spmd

    i = {n: np.asarray(v) for n, v in inputs.items()}
    g = lambda n: i[n]
    wqkv, sw, bq = g("L0_attn_w_qkv"), g("L0_attn_sw_qkv"), g("L0_attn_b_qkv")
    wq, wk, wv = (wqkv[C * n:C * n + C] for n in range(3))

    def pad_scale(s):
        z = np.ones((HEADS, 32), s.dtype)
        z[:, 0:DH] = s.reshape(HEADS, DH)
        return z.reshape(-1)

    w1 = np.moveaxis(g("L0_ffn_w1"), 0, 1)
    w1 = np.concatenate([expert_columns(w1), g("L0_ffn_gate_w").T], axis=1)
    b1 = np.concatenate([expert_columns(g("L0_ffn_b1")), g("L0_ffn_gate_b")])[None, :]
    w2 = g("L0_ffn_w2").reshape(EXPERTS // 2, 2, C, C)
    w2 = np.concatenate([w2[:, 0, 0:128], w2[:, 1, 0:128], w2[:, 0, 128:C], w2[:, 1, 128:C]], axis=1)
    w2 = w2.reshape(TILES, 128, C).transpose(1, 0, 2)
    wp = pad_heads(g("L0_attn_w_proj").T).reshape(3, 128, C).transpose(1, 0, 2)
    arrays = {
        "x": g("x").reshape(BATCH, SEQ * C),
        "tokw": g("L0_tok_w"),
        "scal": np.concatenate([g("L0_attn_s_a1"), g("L0_attn_s_attn"), g("L0_attn_s_a2"), g("L0_attn_s_a3")])[None, :],
        "wqk": rows_128_64(np.concatenate([pad_heads(wq), pad_heads(wk), wv]).T),
        "sw_row": np.concatenate([pad_scale(sw[0:C]), pad_scale(sw[C:2 * C]), sw[2 * C:]])[None, :],
        "bv_row": bq[2 * C:][None, :],
        "wp": wp,
        "sp_row": g("L0_attn_sw_proj")[None, :],
        "bp_row": g("L0_attn_b_proj")[None, :],
        "lnscale": np.stack([g("L0_ffn_scale")[0:128], np.concatenate([g("L0_ffn_scale")[128:192]] * 2)], axis=1),
        "b2": g("L0_ffn_b2"),
        "w2": w2,
        "w1": rows_128_64(w1),
        "b1": b1,
        **constants(),
    }

    def cols(v):
        return np.concatenate([pad_heads(v[0:C]), pad_heads(v[C:2 * C])]).reshape(6, 128).T
    arrays["sw_col"], arrays["b_col"] = cols(sw), cols(bq)
    arrays = {n: np.ascontiguousarray(v) for n, v in arrays.items()}

    nc = bacc.Bacc("TRN2", target_bir_lowering=False, num_devices=1)
    aps = {n: nc.dram_tensor(f"in_{n}", v.shape, mybir.dt.from_np(v.dtype), kind="ExternalInput").ap()
           for n, v in arrays.items()}
    aps["out"] = nc.dram_tensor("out_0", (BATCH, TOK, C), mybir.dt.float32, kind="ExternalOutput").ap()
    build(nc, aps)
    r = run_bass_kernel_spmd(nc, [{f"in_{n}": v for n, v in arrays.items()}], core_ids=[0])
    return r.results[0]["out_0"]
```
